# Optimizing a Trainium2 kernel written in Bass

```python
import numpy as np
import jax
import jax.numpy as jnp

def _softmax(x, axis=-1):
    return jax.nn.softmax(x, axis=axis)

def _gelu(x):
    return jax.nn.gelu(x, approximate=True)

def _silu(x):
    return jax.nn.silu(x)

def _sigmoid(x):
    return jax.nn.sigmoid(x)

def _layernorm(x, axis=-1, eps=1e-05):
    m = jnp.mean(x, axis=axis, keepdims=True)
    v = jnp.var(x, axis=axis, keepdims=True)
    return (x - m) / jnp.sqrt(v + eps)

def _scatter_add(tgt, idx, src, axis=0):
    return tgt.at[idx].add(src)

def _segment_sum(src, seg, n):
    return jax.ops.segment_sum(src, seg, n)
kernel_name = 'mk_vit_tower_postln_d1_tok_img256_r4_4946d8'

def setup_inputs(seed: int=0):
    np.random.seed(seed)
    _w = jnp.asarray

    def _rec_inputs():
        import jax
        import jax.numpy as jnp
        _rk = jax.random.key(seed)
        x = -0.000928989 + 1.00043 * jax.random.normal(jax.random.fold_in(_rk, 1), (32, 64, 64, 1), jnp.float32)
        return x
    x = _rec_inputs()

    def _L0_tok_setup():
        import jax, jax.numpy as jnp
        import numpy as np
        L = 4
        M1 = 12
        M2 = 12
        BN_EPS = 1e-05

        def _fourier_layer(v, W1, W2):
            B, C, Sx, Sy = v.shape
            x_ft = jnp.fft.rfft2(v)
            out1 = jnp.einsum('bixy,ioxy->boxy', x_ft[:, :, :M1, :M2], W1)
            out2 = jnp.einsum('bixy,ioxy->boxy', x_ft[:, :, -M1:, :M2], W2)
            out_ft = jnp.zeros((B, C, Sx, Sy // 2 + 1), jnp.complex64)
            out_ft = out_ft.at[:, :, :M1, :M2].set(out1)
            out_ft = out_ft.at[:, :, Sx - M1:, :M2].set(out2)
            return jnp.fft.irfft2(out_ft, s=(Sx, Sy))
        key = jax.random.key(seed)
        ks = jax.random.split(key, 10)
        B, S, d_a, d_v, d_u = (16, 64, 3, 32, 1)
        return {'x': jax.random.normal(ks[0], (B, S, S, 1), jnp.float32), 'p_w': jax.random.normal(ks[1], (d_a, d_v), jnp.float32) * 0.3, 'p_b': jax.random.normal(ks[2], (d_v,), jnp.float32) * 0.1, 'fw1': jax.random.normal(ks[3], (L, d_v, d_v, M1, M2, 2), jnp.float32) * (1.0 / d_v), 'fw2': jax.random.normal(ks[4], (L, d_v, d_v, M1, M2, 2), jnp.float32) * (1.0 / d_v), 'w_w': jax.random.normal(ks[5], (L, d_v, d_v), jnp.float32) * (1.0 / np.sqrt(d_v)), 'w_b': jax.random.normal(ks[6], (L, d_v), jnp.float32) * 0.1, 'bn_g': jnp.ones((L, d_v), jnp.float32), 'bn_b': jnp.zeros((L, d_v), jnp.float32), 'q_w': jax.random.normal(ks[7], (d_v, d_u), jnp.float32) * 0.3, 'q_b': jax.random.normal(ks[8], (d_u,), jnp.float32) * 0.1}
    _L0_tok_all = _L0_tok_setup()
    _L0_tok_in = {k: v for k, v in _L0_tok_all.items() if k in ('p_w', 'p_b', 'fw1', 'fw2', 'w_w', 'w_b', 'bn_g', 'bn_b', 'q_w', 'q_b')}
    del _L0_tok_all

    def _L0_attn_setup():
        import jax, jax.numpy as jnp
        import numpy as np
        EMB, HEADS, DEPTH, SEQ, BATCH = (64, 8, 4, 2048, 4)
        DH = EMB // HEADS
        FF = 4 * EMB
        EPS = 1e-05

        def _layernorm(x, g, b):
            mu = x.mean(-1, keepdims=True)
            var = ((x - mu) ** 2).mean(-1, keepdims=True)
            return (x - mu) * jax.lax.rsqrt(var + EPS) * g + b

        def _linear_attn(x, Wq, Wk, Wv, Wo, bo):
            b, n, dm = x.shape
            split = lambda t: t.reshape(b, n, HEADS, DH).transpose(0, 2, 1, 3)
            scale = DH ** (-0.25)
            q = jax.nn.softmax(split(x @ Wq) * scale, axis=-1)
            k = jax.nn.softmax(split(x @ Wk) * scale, axis=-2)
            v = split(x @ Wv)
            context = jnp.einsum('bhnd,bhne->bhde', k, v)
            out = jnp.einsum('bhnd,bhde->bhne', q, context)
            out = out.transpose(0, 2, 1, 3).reshape(b, n, dm)
            return out @ Wo + bo

        def _forward(x, Wq, Wk, Wv, Wo, bo, ln1_g, ln1_b, W1, b1, W2, b2, ln2_g, ln2_b):
            for i in range(DEPTH):
                h = _layernorm(x, ln1_g[i], ln1_b[i])
                x = x + _linear_attn(h, Wq[i], Wk[i], Wv[i], Wo[i], bo[i])
                h = _layernorm(x, ln2_g[i], ln2_b[i])
                x = x + (jax.nn.gelu(h @ W1[i] + b1[i], approximate=False) @ W2[i] + b2[i])
            return x
        key = jax.random.key(seed)
        ks = jax.random.split(key, 8)
        w = lambda k, shape: jax.random.normal(k, shape, dtype=jnp.float32) * 0.02
        D = DEPTH
        return {'x': jax.random.normal(ks[0], (BATCH, SEQ, EMB), dtype=jnp.float32), 'Wq': w(ks[1], (D, EMB, EMB)), 'Wk': w(ks[2], (D, EMB, EMB)), 'Wv': w(ks[3], (D, EMB, EMB)), 'Wo': w(ks[4], (D, EMB, EMB)), 'bo': jnp.zeros((D, EMB), jnp.float32), 'ln1_g': jnp.ones((D, EMB), jnp.float32), 'ln1_b': jnp.zeros((D, EMB), jnp.float32), 'W1': w(ks[5], (D, EMB, FF)), 'b1': jnp.zeros((D, FF), jnp.float32), 'W2': w(ks[6], (D, FF, EMB)), 'b2': jnp.zeros((D, EMB), jnp.float32), 'ln2_g': jnp.ones((D, EMB), jnp.float32), 'ln2_b': jnp.zeros((D, EMB), jnp.float32)}
    _L0_attn_all = _L0_attn_setup()
    _L0_attn_in = {k: v for k, v in _L0_attn_all.items() if k in ('Wq', 'Wk', 'Wv', 'Wo', 'bo', 'ln1_g', 'ln1_b', 'W1', 'b1', 'W2', 'b2', 'ln2_g', 'ln2_b')}
    del _L0_attn_all

    def _L0_ffn_setup():
        import jax, jax.numpy as jnp
        import numpy as np
        B, A = (1024, 8)
        IN, OUT = (64, 64)
        SH1, SH2 = (64, 128)
        EH1, EH2 = (128, 64)
        E, TOPK = (4, 2)

        def _shared_mlp(x, W1, b1, W2, b2, W3, b3):
            h = jax.nn.relu(x @ W1 + b1)
            h = jax.nn.relu(h @ W2 + b2)
            return h @ W3 + b3

        def _experts_mlp(x, eW1, eb1, eW2, eb2, eW3, eb3):
            h = jax.nn.relu(jnp.einsum('baf,efh->ebah', x, eW1) + eb1[:, None, None, :])
            h = jax.nn.relu(jnp.einsum('ebah,ehg->ebag', h, eW2) + eb2[:, None, None, :])
            o = jnp.einsum('ebag,ego->ebao', h, eW3) + eb3[:, None, None, :]
            return jnp.moveaxis(o, 0, -1)
        key = jax.random.key(seed)
        ks = jax.random.split(key, 16)
        s = 0.05
        return {'x': jax.random.normal(ks[0], (B, A, IN), jnp.float32), 'sW1': jax.random.normal(ks[1], (IN, SH1), jnp.float32) * s, 'sb1': jnp.zeros((SH1,), jnp.float32), 'sW2': jax.random.normal(ks[2], (SH1, SH2), jnp.float32) * s, 'sb2': jnp.zeros((SH2,), jnp.float32), 'sW3': jax.random.normal(ks[3], (SH2, OUT), jnp.float32) * s, 'sb3': jnp.zeros((OUT,), jnp.float32), 'eW1': jax.random.normal(ks[4], (E, IN, EH1), jnp.float32) * s, 'eb1': jnp.zeros((E, EH1), jnp.float32), 'eW2': jax.random.normal(ks[5], (E, EH1, EH2), jnp.float32) * s, 'eb2': jnp.zeros((E, EH2), jnp.float32), 'eW3': jax.random.normal(ks[6], (E, EH2, OUT), jnp.float32) * s, 'eb3': jnp.zeros((E, OUT), jnp.float32), 'gW': jax.random.normal(ks[7], (IN, E), jnp.float32) * s, 'gb': jnp.zeros((E,), jnp.float32)}
    _L0_ffn_all = _L0_ffn_setup()
    _L0_ffn_in = {k: v for k, v in _L0_ffn_all.items() if k in ('sW1', 'sb1', 'sW2', 'sb2', 'sW3', 'sb3', 'eW1', 'eb1', 'eW2', 'eb2', 'eW3', 'eb3', 'gW', 'gb')}
    del _L0_ffn_all
    return {'x': x, 'L0_tok_p_w': _L0_tok_in['p_w'], 'L0_tok_p_b': _L0_tok_in['p_b'], 'L0_tok_fw1': _L0_tok_in['fw1'], 'L0_tok_fw2': _L0_tok_in['fw2'], 'L0_tok_w_w': _L0_tok_in['w_w'], 'L0_tok_w_b': _L0_tok_in['w_b'], 'L0_tok_bn_g': _L0_tok_in['bn_g'], 'L0_tok_bn_b': _L0_tok_in['bn_b'], 'L0_tok_q_w': _L0_tok_in['q_w'], 'L0_tok_q_b': _L0_tok_in['q_b'], 'L0_attn_Wq': _L0_attn_in['Wq'], 'L0_attn_Wk': _L0_attn_in['Wk'], 'L0_attn_Wv': _L0_attn_in['Wv'], 'L0_attn_Wo': _L0_attn_in['Wo'], 'L0_attn_bo': _L0_attn_in['bo'], 'L0_attn_ln1_g': _L0_attn_in['ln1_g'], 'L0_attn_ln1_b': _L0_attn_in['ln1_b'], 'L0_attn_W1': _L0_attn_in['W1'], 'L0_attn_b1': _L0_attn_in['b1'], 'L0_attn_W2': _L0_attn_in['W2'], 'L0_attn_b2': _L0_attn_in['b2'], 'L0_attn_ln2_g': _L0_attn_in['ln2_g'], 'L0_attn_ln2_b': _L0_attn_in['ln2_b'], 'L0_ffn_sW1': _L0_ffn_in['sW1'], 'L0_ffn_sb1': _L0_ffn_in['sb1'], 'L0_ffn_sW2': _L0_ffn_in['sW2'], 'L0_ffn_sb2': _L0_ffn_in['sb2'], 'L0_ffn_sW3': _L0_ffn_in['sW3'], 'L0_ffn_sb3': _L0_ffn_in['sb3'], 'L0_ffn_eW1': _L0_ffn_in['eW1'], 'L0_ffn_eb1': _L0_ffn_in['eb1'], 'L0_ffn_eW2': _L0_ffn_in['eW2'], 'L0_ffn_eb2': _L0_ffn_in['eb2'], 'L0_ffn_eW3': _L0_ffn_in['eW3'], 'L0_ffn_eb3': _L0_ffn_in['eb3'], 'L0_ffn_gW': _L0_ffn_in['gW'], 'L0_ffn_gb': _L0_ffn_in['gb']}

def reference(x, L0_tok_p_w, L0_tok_p_b, L0_tok_fw1, L0_tok_fw2, L0_tok_w_w, L0_tok_w_b, L0_tok_bn_g, L0_tok_bn_b, L0_tok_q_w, L0_tok_q_b, L0_attn_Wq, L0_attn_Wk, L0_attn_Wv, L0_attn_Wo, L0_attn_bo, L0_attn_ln1_g, L0_attn_ln1_b, L0_attn_W1, L0_attn_b1, L0_attn_W2, L0_attn_b2, L0_attn_ln2_g, L0_attn_ln2_b, L0_ffn_sW1, L0_ffn_sb1, L0_ffn_sW2, L0_ffn_sb2, L0_ffn_sW3, L0_ffn_sb3, L0_ffn_eW1, L0_ffn_eb1, L0_ffn_eW2, L0_ffn_eb2, L0_ffn_eW3, L0_ffn_eb3, L0_ffn_gW, L0_ffn_gb):
    import jax
    import jax.numpy as jnp

    def _L0_tok_ref(x, p_w, p_b, fw1, fw2, w_w, w_b, bn_g, bn_b, q_w, q_b):
        import jax, jax.numpy as jnp
        import numpy as np
        L = 4
        M1 = 12
        M2 = 12
        BN_EPS = 1e-05

        def _fourier_layer(v, W1, W2):
            B, C, Sx, Sy = v.shape
            x_ft = jnp.fft.rfft2(v)
            out1 = jnp.einsum('bixy,ioxy->boxy', x_ft[:, :, :M1, :M2], W1)
            out2 = jnp.einsum('bixy,ioxy->boxy', x_ft[:, :, -M1:, :M2], W2)
            out_ft = jnp.zeros((B, C, Sx, Sy // 2 + 1), jnp.complex64)
            out_ft = out_ft.at[:, :, :M1, :M2].set(out1)
            out_ft = out_ft.at[:, :, Sx - M1:, :M2].set(out2)
            return jnp.fft.irfft2(out_ft, s=(Sx, Sy))
        B, Sx, Sy, _ = x.shape
        gx = jnp.broadcast_to(jnp.linspace(0.0, 1.0, Sx, dtype=jnp.float32)[None, :, None, None], (B, Sx, Sy, 1))
        gy = jnp.broadcast_to(jnp.linspace(0.0, 1.0, Sy, dtype=jnp.float32)[None, None, :, None], (B, Sx, Sy, 1))
        h = jnp.concatenate([x, gx, gy], axis=-1)
        v = h @ p_w + p_b
        v = jnp.transpose(v, (0, 3, 1, 2))
        for i in range(L):
            W1 = fw1[i, ..., 0] + 1j * fw1[i, ..., 1]
            W2 = fw2[i, ..., 0] + 1j * fw2[i, ..., 1]
            x1 = _fourier_layer(v, W1, W2)
            x2 = jnp.einsum('bcxy,cd->bdxy', v, w_w[i]) + w_b[i][None, :, None, None]
            v = x1 + x2
            mean = jnp.mean(v, axis=(0, 2, 3), keepdims=True)
            var = jnp.var(v, axis=(0, 2, 3), keepdims=True)
            v = (v - mean) * jax.lax.rsqrt(var + BN_EPS)
            v = v * bn_g[i][None, :, None, None] + bn_b[i][None, :, None, None]
            if i < L - 1:
                v = jax.nn.relu(v)
        out = jnp.einsum('bcxy,cu->bxyu', v, q_w) + q_b
        return jnp.squeeze(out)

    def _L0_attn_ref(x, Wq, Wk, Wv, Wo, bo, ln1_g, ln1_b, W1, b1, W2, b2, ln2_g, ln2_b):
        import jax, jax.numpy as jnp
        import numpy as np
        EMB, HEADS, DEPTH, SEQ, BATCH = (64, 8, 4, 2048, 4)
        DH = EMB // HEADS
        FF = 4 * EMB
        EPS = 1e-05

        def _layernorm(x, g, b):
            mu = x.mean(-1, keepdims=True)
            var = ((x - mu) ** 2).mean(-1, keepdims=True)
            return (x - mu) * jax.lax.rsqrt(var + EPS) * g + b

        def _linear_attn(x, Wq, Wk, Wv, Wo, bo):
            b, n, dm = x.shape
            split = lambda t: t.reshape(b, n, HEADS, DH).transpose(0, 2, 1, 3)
            scale = DH ** (-0.25)
            q = jax.nn.softmax(split(x @ Wq) * scale, axis=-1)
            k = jax.nn.softmax(split(x @ Wk) * scale, axis=-2)
            v = split(x @ Wv)
            context = jnp.einsum('bhnd,bhne->bhde', k, v)
            out = jnp.einsum('bhnd,bhde->bhne', q, context)
            out = out.transpose(0, 2, 1, 3).reshape(b, n, dm)
            return out @ Wo + bo

        def _forward(x, Wq, Wk, Wv, Wo, bo, ln1_g, ln1_b, W1, b1, W2, b2, ln2_g, ln2_b):
            for i in range(DEPTH):
                h = _layernorm(x, ln1_g[i], ln1_b[i])
                x = x + _linear_attn(h, Wq[i], Wk[i], Wv[i], Wo[i], bo[i])
                h = _layernorm(x, ln2_g[i], ln2_b[i])
                x = x + (jax.nn.gelu(h @ W1[i] + b1[i], approximate=False) @ W2[i] + b2[i])
            return x
        return _forward(x, Wq, Wk, Wv, Wo, bo, ln1_g, ln1_b, W1, b1, W2, b2, ln2_g, ln2_b)

    def _L0_ffn_ref(x, sW1, sb1, sW2, sb2, sW3, sb3, eW1, eb1, eW2, eb2, eW3, eb3, gW, gb):
        import jax, jax.numpy as jnp
        import numpy as np
        B, A = (1024, 8)
        IN, OUT = (64, 64)
        SH1, SH2 = (64, 128)
        EH1, EH2 = (128, 64)
        E, TOPK = (4, 2)

        def _shared_mlp(x, W1, b1, W2, b2, W3, b3):
            h = jax.nn.relu(x @ W1 + b1)
            h = jax.nn.relu(h @ W2 + b2)
            return h @ W3 + b3

        def _experts_mlp(x, eW1, eb1, eW2, eb2, eW3, eb3):
            h = jax.nn.relu(jnp.einsum('baf,efh->ebah', x, eW1) + eb1[:, None, None, :])
            h = jax.nn.relu(jnp.einsum('ebah,ehg->ebag', h, eW2) + eb2[:, None, None, :])
            o = jnp.einsum('ebag,ego->ebao', h, eW3) + eb3[:, None, None, :]
            return jnp.moveaxis(o, 0, -1)
        all_out = _experts_mlp(x, eW1, eb1, eW2, eb2, eW3, eb3)
        shared = _shared_mlp(x, sW1, sb1, sW2, sb2, sW3, sb3)
        gates = jax.nn.softmax(x @ gW + gb, axis=-1)
        topv, topi = jax.lax.top_k(gates, TOPK)
        topw = jax.nn.softmax(topv, axis=-1)
        sel = jnp.take_along_axis(all_out, topi[:, :, None, :], axis=-1)
        gated = jnp.sum(sel * topw[:, :, None, :], axis=-1)
        return shared + gated
    h = _L0_tok_ref(x, L0_tok_p_w, L0_tok_p_b, L0_tok_fw1, L0_tok_fw2, L0_tok_w_w, L0_tok_w_b, L0_tok_bn_g, L0_tok_bn_b, L0_tok_q_w, L0_tok_q_b)
    h = _layernorm(h + _L0_attn_ref(h, L0_attn_Wq, L0_attn_Wk, L0_attn_Wv, L0_attn_Wo, L0_attn_bo, L0_attn_ln1_g, L0_attn_ln1_b, L0_attn_W1, L0_attn_b1, L0_attn_W2, L0_attn_b2, L0_attn_ln2_g, L0_attn_ln2_b), axis=-1)
    h = _layernorm(h + _L0_ffn_ref(h, L0_ffn_sW1, L0_ffn_sb1, L0_ffn_sW2, L0_ffn_sb2, L0_ffn_sW3, L0_ffn_sb3, L0_ffn_eW1, L0_ffn_eb1, L0_ffn_eW2, L0_ffn_eb2, L0_ffn_eW3, L0_ffn_eb3, L0_ffn_gW, L0_ffn_gb), axis=-1)
    return h

_drawn_inputs = setup_inputs


def setup_inputs(seed=0):
    import zlib

    import numpy as np

    out = dict(_drawn_inputs(seed))
    spreads = {'L0_tok_bn_g': (1.0, 0.2),
     'L0_tok_bn_b': (0.0, 0.1),
     'L0_attn_bo': (0.0, 0.1),
     'L0_attn_ln1_g': (1.0, 0.6),
     'L0_attn_ln1_b': (0.0, 0.8),
     'L0_attn_b1': (0.0, 0.62),
     'L0_attn_b2': (0.0, 0.1),
     'L0_attn_ln2_g': (1.0, 0.6),
     'L0_attn_ln2_b': (0.0, 0.8),
     'L0_ffn_sb1': (0.0, 0.8),
     'L0_ffn_sb2': (0.0, 0.1),
     'L0_ffn_sb3': (0.0, 0.1),
     'L0_ffn_eb1': (0.0, 0.8),
     'L0_ffn_eb2': (0.0, 0.551),
     'L0_ffn_eb3': (0.0, 0.1),
     'L0_ffn_gb': (0.0, 0.312)}
    factors = {'L0_tok_p_b': 8.0,
     'L0_tok_w_b': 8.0,
     'L0_attn_Wq': 8.0,
     'L0_attn_Wk': 8.0,
     'L0_attn_Wv': 6.052,
     'L0_attn_Wo': 6.668,
     'L0_attn_W1': 2.689,
     'L0_ffn_eW1': 2.77}
    for name, (base, spread) in spreads.items():
        noise = np.random.default_rng([zlib.crc32(name.encode()), seed]).standard_normal(out[name].shape)
        drawn = base * np.exp(spread * noise) if base else spread * noise
        out[name] = jnp.asarray(drawn.astype(out[name].dtype))
    for name, factor in factors.items():
        out[name] = (out[name] * factor).astype(out[name].dtype)
    return out
```

```python
import numpy as np
import concourse.bass as bass
from concourse import mybir
from contextlib import ExitStack

LAYERS = 4
BATCH = 32
S = 64
CH = 32
MODES = 12
Q = 32
P = 128
PAIRS = BATCH // 2
KXJ = 6
EPS = 1e-5


def constants():
    two_pi = 2.0 * np.pi / S
    y = np.arange(S)
    ky = np.arange(MODES)
    cy = np.cos(two_pi * np.outer(y, ky))
    sy = np.sin(two_pi * np.outer(y, ky))
    fwd_y = np.zeros((2, S, 2, Q))
    for b in range(2):
        fwd_y[b, :, b, 0:MODES] = cy
        fwd_y[b, :, b, MODES:2 * MODES] = -sy
    freq = np.array([[KXJ * j + k if j < 2 else S - MODES + KXJ * (j - 2) + k for k in range(KXJ)]
                     for j in range(4)])
    x = np.arange(S)
    cx = np.cos(two_pi * x[:, None, None] * freq)
    sx = np.sin(two_pi * x[:, None, None] * freq)
    fwd_x = np.zeros((2, 2, 2, Q, 4, Q))
    inv_x = np.zeros((2, 4, Q, 2, 2, Q))
    for xh in range(2):
        c, s = cx[xh * Q:(xh + 1) * Q], sx[xh * Q:(xh + 1) * Q]
        for j in range(4):
            for k in range(KXJ):
                for b in range(2):
                    at = b * MODES + 2 * k
                    re, im = 2 * (j // 2), 2 * (j // 2) + 1
                    col = 2 * (KXJ * (j % 2) + k) + b
                    fwd_x[0, xh, b, :, re, col] = c[:, j, k]
                    fwd_x[0, xh, b, :, im, col] = -s[:, j, k]
                    fwd_x[1, xh, b, :, re, col] = s[:, j, k]
                    fwd_x[1, xh, b, :, im, col] = c[:, j, k]
                    inv_x[b, j, at, xh, 0] = c[:, j, k]
                    inv_x[b, j, at, xh, 1] = s[:, j, k]
                    inv_x[b, j, at + 1, xh, 0] = -s[:, j, k]
                    inv_x[b, j, at + 1, xh, 1] = c[:, j, k]
    weight = np.where(ky == 0, 1.0, 2.0) / (S * S)
    inv_y = np.zeros((2, 2, 2, Q, 2, S))
    for xh in range(2):
        for b in range(2):
            rows = slice(b * MODES, (b + 1) * MODES)
            inv_y[xh, xh, 0, rows, b] = (weight * cy).T
            inv_y[xh, xh, 1, rows, b] = -(weight * sy).T
    average = np.tile(np.eye(CH), (4, 4)) / 4.0
    first = np.zeros((P, P))
    first[0:CH] = 1.0
    pick = np.zeros((P, Q))
    for q in range(4):
        pick[q * Q:(q + 1) * Q, q] = 1.0
    table = np.concatenate([
        fwd_y.reshape(P, 2 * Q),
        fwd_x.reshape(2, P, P).transpose(1, 0, 2).reshape(P, 2 * P),
        inv_x.reshape(2, P, P).transpose(1, 0, 2).reshape(P, 2 * P),
        inv_y.reshape(2, P, P).transpose(1, 0, 2).reshape(P, 2 * P),
        average, first, pick], axis=1).astype(np.float32)
    grid = np.zeros((4, Q, S, Q), np.float32)
    line = np.linspace(0.0, 1.0, S, dtype=np.float32)
    for q in range(4):
        grid[q, 1] = line[:, None]
        grid[q, 2] = line[None, (q % 2) * Q:(q % 2) * Q + Q]
        grid[q, 3] = 1.0
    return table, grid.reshape(P, S * Q)


def tower_layout(x, p_w, p_b, fw1, fw2, w_w, w_b, bn_g, bn_b, q_w, q_b):
    pixels = x.reshape(PAIRS, 2, S, 2, Q).transpose(1, 3, 0, 2, 4).reshape(4, PAIRS * S * Q)
    lift = np.zeros((4, Q, 4, CH), np.float32)
    conv = np.zeros((4, CH, LAYERS, 4, CH), np.float32)
    for q in range(4):
        lift[q, 0:3, q] = p_w
        lift[q, 3, q] = p_b
        conv[q, :, :, q] = w_w.transpose(1, 0, 2)
    params = np.concatenate([w_b.T, bn_g.T, bn_b.T, q_w, np.broadcast_to(q_b, (CH, 1))], axis=1)
    parts = np.stack([fw1, fw2]).transpose(1, 5, 0, 2, 4, 6, 3)
    modes = np.stack([parts, parts[..., ::-1, :]], axis=3).reshape(LAYERS * MODES, P, 2 * MODES * CH)
    weights = np.concatenate([lift.reshape(P, P), conv.reshape(P, LAYERS * P), np.tile(params, (4, 1))], axis=1)
    return [np.ascontiguousarray(a) for a in (pixels, weights, modes)]


def tower_kernel(nc, pixels, weights, modes, table, grid, tower_out):
    f32 = mybir.dt.float32
    ALU = mybir.AluOpType
    ACT = mybir.ActivationFunctionType
    L = LAYERS
    HALF = (S // 2) * Q
    RBUF = 4
    BLK = 2 * HALF
    HB = Q * CH
    YR = MODES * CH
    OB = S // 2

    with ExitStack() as ctx:
        def sb(name, shape):
            return ctx.enter_context(nc.sbuf_tensor(name, shape, f32))

        def sem(name):
            return ctx.enter_context(nc.semaphore(name))

        V = sb("V", [P, PAIRS * BLK])
        spec = sb("spec", [P, MODES, PAIRS * CH])
        r_ky = sb("r_ky", [P, RBUF, MODES, 2, CH])
        arena = sb("arena", [P, 8 * HB])
        tab = sb("tab", [P, 1120])
        m_proj = sb("m_proj", [P, Q])
        wts = sb("wts", [P, P + L * P + 3 * L + 2])
        sums = sb("sums", [P, 2 * PAIRS])
        squares = sb("squares", [P, 2 * PAIRS])
        small = sb("small", [P, 24])
        ps = ctx.enter_context(nc.psum_tensor("ps", [P, 4096], f32))

        fwd_y = tab[:, 0:64]
        fwd_x = [tab[:, 64 + P * i:64 + P * (i + 1)] for i in range(2)]
        inv_x = [tab[:, 320 + P * i:320 + P * (i + 1)] for i in range(2)]
        inv_y = [tab[:, 576 + P * i:576 + P * (i + 1)] for i in range(2)]
        average = tab[:, 832:960]
        first = tab[:, 960:1088]
        pick = tab[:, 1088:1120]
        A = [arena[:, HB * i:HB * (i + 1)] for i in range(8)]
        f_act, f_tr, f_yt = A[0:2], A[2:4], A[4]
        m_in = [arena[:, 512 * i:512 * (i + 1)] for i in range(2)]
        m_out = A[2:4]
        b_act, b_gs, b_gt, b_x1, b_sq = A[0:2], A[2], (A[3], A[6]), A[4:6], A[7]
        lift_w = wts[:, 0:P]
        conv_w = [wts[:, P * (l + 1):P * (l + 2)] for l in range(L)]
        at = P * (L + 1)
        w_bias, bn_gain, bn_bias = ([wts[:, at + L * k + l:at + L * k + l + 1] for l in range(L)] for k in range(3))
        q_gain, q_bias = wts[:, at + 3 * L:at + 3 * L + 1], wts[:, at + 3 * L + 1:at + 3 * L + 2]
        flat = spec[:, :, :].rearrange("p k n -> p (k n)")
        feat = [flat[:, BLK * i:BLK * (i + 1)] for i in range(2)]

        def bank(i, n=1):
            return ps[:, 512 * i:512 * (i + n)]

        s_const = sem("s_const")
        s_feat = [sem("s_feat0"), sem("s_feat1")]
        s_lift = sem("s_lift")
        s_lifted = sem("s_lifted")
        s_fact = sem("s_fact")
        s_ftr = sem("s_ftr")
        s_fy = sem("s_fy")
        s_fyt = sem("s_fyt")
        s_fx = sem("s_fx")
        s_spec = sem("s_spec")
        s_rload = [sem(f"s_rload{i}") for i in range(RBUF)]
        s_rky = sem("s_rky")
        s_min = sem("s_min")
        s_mix = sem("s_mix")
        s_mout = sem("s_mout")
        s_msp = sem("s_msp")
        s_gx = sem("s_gx")
        s_gs = sem("s_gs")
        s_gt = sem("s_gt")
        s_bact = sem("s_bact")
        s_iy = sem("s_iy")
        s_x1 = sem("s_x1")
        s_conv = sem("s_conv")
        s_v = sem("s_v")
        s_squares = sem("s_squares")
        s_pivot = sem("s_pivot")
        s_avg = sem("s_avg")
        s_bn = sem("s_bn")
        s_sqrt = sem("s_sqrt")
        s_norm = sem("s_norm")
        s_chain = sem("s_chain")
        s_out = sem("s_out")
        s_pads = sem("s_pads")
        s_pick = sem("s_pick")
        s_proj = sem("s_proj")
        s_u = sem("s_u")

        def at_least(eng, s, n):
            if not isinstance(n, int) or n > 0:
                eng.wait_ge(s, n)

        block = ctx.enter_context(nc.Block())

        CHAIN_AT_PROJ = 14 * L + 2

        @block.sync
        def _(sp):
            sp.dma_start(wts[:, :], weights).then_inc(s_const, 16)
            for i in range(2):
                sp.dma_start(feat[i], grid).then_inc(s_feat[i], 16)

            def load_pixels(i, par):
                for q in range(4):
                    sp.dma_start(feat[par][Q * q:Q * q + 1, :], pixels[q:q + 1, bass.ds(BLK * i, BLK)]).then_inc(s_feat[par], 16)

            def load_modes(n):
                if n >= RBUF:
                    sp.wait_ge(s_mix, n - RBUF + 1)
                sp.dma_start(r_ky[:, n % RBUF].rearrange("p k s o -> p (k s o)"), modes[n]).then_inc(s_rload[n % RBUF], 16)

            for i in range(2):
                sp.wait_ge(s_feat[i], 16)
                load_pixels(i, i)
            sp.dma_start(tab[:, :], table).then_inc(s_const, 16)
            for n in range(RBUF):
                load_modes(n)
            with sp.Fori(1, PAIRS // 2) as it:
                for par in range(2):
                    sp.wait_ge(s_lift, 8 * it + 4 * par - 4)
                    load_pixels(2 * it + par, par)
            for n in range(RBUF, L * MODES):
                load_modes(n)
            sp.wait_ge(s_u, PAIRS)
            for k in range(4):
                src = V[Q * k:Q * k + 4, :].rearrange("p (i n) -> p i n", i=PAIRS)[:, :, 0:512]
                sp.dma_start(tower_out[4 * k:4 * k + 4, :].rearrange("q (i n) -> q i n", i=PAIRS), src).then_inc(s_out, 16)
            sp.wait_ge(s_out, 64)

        @block.gpsimd
        def _(pool):
            for n in range(L * MODES):
                pool.wait_ge(s_rload[n % RBUF], 16 * (n // RBUF + 1))
                for jj in range(2):
                    im = r_ky[64 * jj + Q:64 * (jj + 1), n % RBUF, :, 0, :]
                    nc.gpsimd.tensor_scalar(im, im, -1.0, 0.0, ALU.mult, ALU.add).then_inc(s_rky, 1)

        @block.scalar
        def _(act):
            with act.Fori(0, PAIRS // 2) as it:
                for par in range(2):
                    for k in range(4):
                        act.wait_ge(s_lift, 8 * it + 4 * par + k + 1)
                        nc.scalar.copy(V[:, bass.ds(2 * BLK * it + BLK * par + 512 * k, 512)],
                                       bank(4 * par + k)).then_inc(s_lifted, 1)
            for l in range(L):
                func = ACT.Relu if l else ACT.Identity
                scale = small[:, 0:1] if l else 1.0
                bias = small[:, 1:2] if l else 0.0
                act.wait_ge(s_lifted, 4 * PAIRS)
                if l:
                    act.wait_ge(s_norm, l)

                def f_activate(n, par):
                    for h in range(2):
                        at_least(act, s_ftr, 2 * n + h - 1 + 2 * PAIRS * l)
                        nc.scalar.activation(f_act[h], V[:, bass.ds(n * BLK + h * HALF, HALF)], func,
                                             bias=bias, scale=scale).then_inc(s_fact, 1)

                def f_store(n, par):
                    act.wait_ge(s_fx, n + 1 + PAIRS * l)
                    nc.scalar.copy(spec[:, :, bass.ds(n * CH, CH)],
                                   bank(4 + par)[:, 0:YR].rearrange("p (k c) -> p k c", c=CH)).then_inc(s_spec, 1)

                f_activate(0, 0)
                f_activate(1, 1)
                with act.Fori(1, PAIRS // 2) as it:
                    for par in range(2):
                        f_activate(2 * it + par, par)
                        f_store(2 * it + par - 2, par)
                f_store(PAIRS - 2, 0)
                f_store(PAIRS - 1, 1)

                act.wait_ge(s_pads, l + 1)
                for ky in range(MODES):
                    n = l * MODES + ky
                    act.wait_ge(s_mix, n + 1)
                    at_least(act, s_msp, n // 2 - 1)
                    for j in range(4):
                        rows = slice(Q * j, Q * (j + 1))
                        out = m_out[(n // 2) % 2][rows].rearrange("p (o s) -> p s o", s=Q)[:, (ky % 2) * MODES:(ky % 2 + 1) * MODES, :]
                        nc.scalar.copy(out, ps[rows, 512 * (4 * (n % 2) + j):512 * (4 * (n % 2) + j) + YR]
                                       .rearrange("p (s o) -> p s o", o=CH)).then_inc(s_mout, 1)

                act.wait_ge(s_msp, (MODES // 2) * (l + 1))

                def b_activate(n, par, h):
                    at_least(act, s_conv, 2 * n + h - 1 + 2 * PAIRS * l)
                    nc.scalar.activation(b_act[h], V[:, bass.ds(n * BLK + h * HALF, HALF)], func,
                                         bias=bias, scale=scale).then_inc(s_bact, 1)

                def b_stage(n, par):
                    act.wait_ge(s_gx, n + 1 + PAIRS * l)
                    at_least(act, s_gt, n + PAIRS * l)
                    for p in range(2):
                        out = b_gs.rearrange("p (o s) -> p s o", s=Q)[:, 0:2 * MODES, :] \
                            .rearrange("p (b k e) o -> p e k b o", b=2, e=2)[:, p]
                        nc.scalar.copy(out, bank(p)[:, 0:YR].rearrange("p (k b o) -> p k b o", b=2, o=CH)).then_inc(s_gs, 1)

                def b_square(n, h):
                    act.wait_ge(s_v, 2 * n + h + 1 + 2 * PAIRS * l)
                    at_least(act, s_squares, 2 * n + h + 2 * PAIRS * l)
                    nc.scalar.activation(b_sq, V[:, bass.ds(n * BLK + h * HALF, HALF)], ACT.Square, bias=small[:, 8:9],
                                         accum_out=squares[:, bass.ds(2 * n + h, 1)]).then_inc(s_squares, 1)

                b_stage(0, 0)
                b_activate(0, 0, 0)
                b_activate(0, 0, 1)
                b_stage(1, 1)
                b_activate(1, 1, 0)
                act.wait_ge(s_pivot, l + 1)
                b_square(0, 0)
                b_activate(1, 1, 1)
                with act.Fori(0, PAIRS // 2 - 1) as it:
                    for par in range(2):
                        n = 2 * it + par
                        b_stage(n + 2, par)
                        b_square(n, 1)
                        b_activate(n + 2, par, 0)
                        b_square(n + 1, 0)
                        b_activate(n + 2, par, 1)
                b_square(PAIRS - 2, 1)
                b_square(PAIRS - 1, 0)
                b_square(PAIRS - 1, 1)
                act.wait_ge(s_bn, 3 * l + 3)
                nc.scalar.activation(small[:, 10:11], small[:, 9:10], ACT.Sqrt).then_inc(s_sqrt, 1)

            act.wait_ge(s_pick, 2)
            for i in range(PAIRS):
                act.wait_ge(s_proj, i + 2)
                nc.scalar.activation(V[:, BLK * i:BLK * i + 512], bank(i % 4), ACT.Identity,
                                     bias=small[:, 14:15], scale=1.0).then_inc(s_u, 1)

        @block.vector
        def _(dve):
            chain = [0]

            def link(ins):
                chain[0] += 1
                ins.then_inc(s_chain, 1)
                dve.wait_ge(s_chain, chain[0])

            for l in range(L):
                def f_transpose(n, par):
                    for h in range(2):
                        dve.wait_ge(s_fact, 2 * n + h + 1 + 2 * PAIRS * l)
                        at_least(dve, s_fy, 2 * n + h - 1 + 2 * PAIRS * l)
                        nc.vector.transpose(f_tr[h], f_act[h]).then_inc(s_ftr, 1)

                def f_spectra(n, par):
                    dve.wait_ge(s_fy, 2 * n + 2 + 2 * PAIRS * l)
                    at_least(dve, s_fx, n + PAIRS * l)
                    nc.vector.transpose(f_yt.rearrange("p (k c) -> p c k", c=CH),
                                        bank(2 * par, 2).rearrange("p (x c) -> p c x", c=CH)).then_inc(s_fyt, 1)

                f_transpose(0, 0)
                f_transpose(1, 1)
                f_spectra(0, 0)
                with dve.Fori(1, PAIRS // 2) as it:
                    for par in range(2):
                        f_transpose(2 * it + par, par)
                        f_spectra(2 * it + par - 1, 1 - par)
                f_spectra(PAIRS - 1, 1)

                for a in m_out:
                    pads = nc.vector.memset(a.rearrange("p (o s) -> p o s", s=Q)[:, :, 2 * MODES:Q], 0.0)
                pads.then_inc(s_pads, 1)

                def mix_in(ky):
                    n = l * MODES + ky
                    at_least(dve, s_mix, n - 1)
                    nc.vector.transpose(m_in[n % 2].rearrange("p (s i) -> p i s", i=PAIRS), spec[:, ky, :]).then_inc(s_min, 1)

                dve.wait_ge(s_spec, PAIRS * (l + 1))
                mix_in(0)
                mix_in(1)
                for ky in range(MODES):
                    if ky + 2 < MODES:
                        mix_in(ky + 2)
                    if ky % 2:
                        n = l * MODES + ky
                        dve.wait_ge(s_mout, 4 * (n + 1))
                        out = spec[:, ky - 1:ky + 1, :].rearrange("p k n -> p (k n)").rearrange("p (b o) -> p o b", o=CH)
                        nc.vector.transpose(out, m_out[(n // 2) % 2]).then_inc(s_msp, 1)

                def g_transpose(n, par):
                    dve.wait_ge(s_gs, 2 * n + 2 + 2 * PAIRS * l)
                    at_least(dve, s_iy, 2 * n - 2 + 2 * PAIRS * l)
                    nc.vector.transpose(b_gt[par].rearrange("p (x o) -> p o x", o=CH), b_gs).then_inc(s_gt, 1)

                def combine(n, h):
                    half = 2 * n + h + 2 * PAIRS * l
                    dve.wait_ge(s_iy, half + 1)
                    nc.vector.transpose(b_x1[h], bank(2, 2)).then_inc(s_x1, 1)
                    dve.wait_ge(s_conv, half + 1)
                    dve.wait_ge(s_x1, half + 1)
                    nc.vector.scalar_tensor_tensor(out=V[:, bass.ds(n * BLK + h * HALF, HALF)], in0=bank(4 + 2 * h, 2),
                                                   scalar=w_bias[l], in1=b_x1[h], op0=ALU.add, op1=ALU.add,
                                                   accum_out=sums[:, bass.ds(2 * n + h, 1)]).then_inc(s_v, 1)

                g_transpose(0, 0)
                combine(0, 0)
                dve.wait_ge(s_v, 2 * PAIRS * l + 1)
                nc.vector.tensor_scalar(small[:, 8:9], sums[:, 0:1], -1.0 / HALF, None, ALU.mult).then_inc(s_pivot, 1)
                g_transpose(1, 1)
                combine(0, 1)
                with dve.Fori(1, PAIRS // 2) as it:
                    for par in range(2):
                        n = 2 * it + par - 1
                        combine(n, 0)
                        g_transpose(n + 1, par)
                        combine(n, 1)
                combine(PAIRS - 1, 0)
                combine(PAIRS - 1, 1)

                dve.wait_ge(s_v, 2 * PAIRS * (l + 1))
                dve.wait_ge(s_pivot, l + 1)
                link(nc.vector.reduce_sum(small[:, 17:18], sums[:, :], mybir.AxisListType.X))
                link(nc.vector.tensor_scalar(small[:, 2:3], small[:, 17:18], 1.0 / (PAIRS * BLK), None, ALU.mult))
                link(nc.vector.tensor_scalar(small[:, 18:19], small[:, 2:3], small[:, 8:9], None, ALU.add))
                link(nc.vector.tensor_tensor(small[:, 19:20], small[:, 18:19], small[:, 18:19], ALU.mult))
                dve.wait_ge(s_squares, 2 * PAIRS * (l + 1))
                link(nc.vector.reduce_sum(small[:, 17:18], squares[:, :], mybir.AxisListType.X))
                nc.vector.scalar_tensor_tensor(out=small[:, 3:4], in0=small[:, 17:18], scalar=1.0 / (PAIRS * BLK),
                                               in1=small[:, 19:20], op0=ALU.mult, op1=ALU.subtract).then_inc(s_bn, 1)
                dve.wait_ge(s_avg, 2 * l + 1)
                dve.wait_ge(s_bn, 3 * l + 1)
                link(nc.vector.tensor_copy(small[:, 5:7], bank(0)[:, 0:2]))
                link(nc.vector.tensor_tensor(small[:, 7:8], small[:, 2:3], small[:, 5:6], ALU.subtract))
                nc.vector.tensor_tensor(small[:, 4:5], small[:, 7:8], small[:, 7:8], ALU.mult).then_inc(s_bn, 1)
                dve.wait_ge(s_avg, 2 * l + 2)
                nc.vector.tensor_scalar(small[:, 9:10], bank(1)[:, 0:1], small[:, 6:7], EPS, ALU.add, ALU.add).then_inc(s_bn, 1)
                dve.wait_ge(s_bn, 3 * l + 3)
                dve.wait_ge(s_sqrt, l + 1)
                link(nc.vector.reciprocal(small[:, 11:12], small[:, 10:11]))
                link(nc.vector.tensor_tensor(small[:, 12:13], small[:, 11:12], small[:, 11:12], ALU.mult))
                link(nc.vector.tensor_tensor(small[:, 13:14], small[:, 12:13], small[:, 9:10], ALU.mult))
                link(nc.vector.tensor_scalar(small[:, 12:13], small[:, 13:14], -0.5, 1.5, ALU.mult, ALU.add))
                link(nc.vector.tensor_tensor(small[:, 13:14], small[:, 12:13], small[:, 11:12], ALU.mult))
                link(nc.vector.tensor_tensor(small[:, 0:1], small[:, 13:14], bn_gain[l], ALU.mult))
                link(nc.vector.tensor_tensor(small[:, 12:13], small[:, 0:1], small[:, 5:6], ALU.mult))
                nc.vector.tensor_tensor(small[:, 1:2], bn_bias[l], small[:, 12:13], ALU.subtract).then_inc(s_norm, 1)
                dve.wait_ge(s_norm, l + 1)

            link(nc.vector.tensor_tensor(small[:, 15:16], small[:, 0:1], q_gain, ALU.mult))
            nc.vector.tensor_scalar(m_proj[:, :], pick, small[:, 15:16], None, ALU.mult).then_inc(s_pick, 1)
            link(nc.vector.tensor_tensor(small[:, 16:17], small[:, 1:2], q_gain, ALU.mult))
            dve.wait_ge(s_proj, 1)
            nc.vector.tensor_scalar(small[:, 14:15], bank(4)[:, 0:1], q_bias, None, ALU.add).then_inc(s_pick, 1)

        @block.tensor
        def _(pe):
            pe.wait_ge(s_const, 32)

            def lift(i, par):
                pe.wait_ge(s_feat[par], 32 * i + 16 + 64 - 32 * par)
                for k in range(4):
                    at_least(pe, s_lifted, 4 * i + k - 7)
                    nc.tensor.matmul(bank(4 * par + k), lift_w, feat[par][:, 512 * k:512 * (k + 1)],
                                     start=True, stop=True).then_inc(s_lift, 1)

            lift(0, 0)
            lift(1, 1)
            with pe.Fori(1, PAIRS // 2) as it:
                for par in range(2):
                    lift(2 * it + par, par)
            for l in range(L):
                def forward_y(n, par):
                    at_least(pe, s_fyt, n - 1 + PAIRS * l)
                    for h in range(2):
                        pe.wait_ge(s_ftr, 2 * n + h + 1 + 2 * PAIRS * l)
                        for k in range(2):
                            last = nc.tensor.matmul(bank(2 * par + k)[64 * h:64 * h + 64, :], fwd_y,
                                                    f_tr[h][:, 512 * k:512 * (k + 1)], start=True, stop=True)
                        last.then_inc(s_fy, 1)

                def forward_x(n, par):
                    pe.wait_ge(s_fyt, n + 1 + PAIRS * l)
                    at_least(pe, s_spec, n - 1 + PAIRS * l)
                    for ri in range(2):
                        last = nc.tensor.matmul(bank(4 + par)[:, 0:YR], fwd_x[ri], f_yt[:, YR * ri:YR * (ri + 1)],
                                                start=ri == 0, stop=ri == 1)
                    last.then_inc(s_fx, 1)

                if l:
                    pe.wait_ge(s_norm, l)
                else:
                    pe.wait_ge(s_lifted, 4 * PAIRS)
                forward_y(0, 0)
                forward_y(1, 1)
                forward_x(0, 0)
                for n in range(2, 4):
                    forward_y(n, n % 2)
                    forward_x(n - 1, (n - 1) % 2)
                with pe.Fori(2, PAIRS // 2) as it:
                    for par in range(2):
                        forward_y(2 * it + par, par)
                        forward_x(2 * it + par - 1, 1 - par)
                forward_x(PAIRS - 1, 1)

                pe.wait_ge(s_spec, PAIRS * (l + 1))
                for ky in range(MODES):
                    n = l * MODES + ky
                    pe.wait_ge(s_min, n + 1)
                    pe.wait_ge(s_rky, 2 * (n + 1))
                    at_least(pe, s_mout, 4 * (n - 1))
                    for kx in range(KXJ):
                        for jh in range(2):
                            for jj in range(2):
                                j, k12 = 2 * jj + jh, KXJ * jh + kx
                                rows = slice(64 * jj, 64 * (jj + 1))
                                at = 512 * (4 * (n % 2) + j) + 2 * CH * kx
                                last = nc.tensor.matmul(ps[Q * j:Q * (j + 1), at:at + 2 * CH],
                                                        m_in[n % 2][rows, Q * k12:Q * (k12 + 1)],
                                                        r_ky[rows, n % RBUF, k12].rearrange("p s o -> p (s o)"),
                                                        start=True, stop=True, tile_position=(64 * jj, Q * j))
                    last.then_inc(s_mix, 1)

                vk = spec[:, :, :].rearrange("p k n -> p (k n)").rearrange("p (k b i o) -> p k b i o", b=2, i=PAIRS, o=CH)

                def inverse_x(n):
                    at_least(pe, s_gs, 2 * n + 2 * PAIRS * l)
                    for p in range(2):
                        last = nc.tensor.matmul(bank(p)[:, 0:YR], inv_x[p], vk[:, :, :, bass.ds(n, 1), :].rearrange("p k b i o -> p k b (i o)"),
                                                start=True, stop=True)
                    last.then_inc(s_gx, 1)

                def pair(n, par):
                    pe.wait_ge(s_gt, n + 1 + PAIRS * l)
                    for h in range(2):
                        half = 2 * n + h + 2 * PAIRS * l
                        at_least(pe, s_x1, half)
                        for k in range(2):
                            last = nc.tensor.matmul(bank(2 + k), inv_y[h], b_gt[par][:, 512 * k:512 * (k + 1)],
                                                    start=True, stop=True)
                        last.then_inc(s_iy, 1)
                        pe.wait_ge(s_bact, half + 1)
                        at_least(pe, s_v, half - 1)
                        for k in range(2):
                            last = nc.tensor.matmul(bank(4 + 2 * h + k), conv_w[l], b_act[h][:, 512 * k:512 * (k + 1)],
                                                    start=True, stop=True)
                        last.then_inc(s_conv, 1)

                pe.wait_ge(s_msp, (MODES // 2) * (l + 1))
                inverse_x(0)
                inverse_x(1)
                pair(0, 0)
                inverse_x(2)
                pair(1, 1)
                with pe.Fori(1, PAIRS // 2 - 1) as it:
                    for par in range(2):
                        inverse_x(2 * it + par + 1)
                        pair(2 * it + par, par)
                inverse_x(PAIRS - 1)
                pair(PAIRS - 2, 0)
                pair(PAIRS - 1, 1)

                pe.wait_ge(s_bn, 3 * l + 1)
                nc.tensor.matmul(bank(0)[:, 0:2], average, small[:, 2:4], start=True, stop=True).then_inc(s_avg, 1)
                pe.wait_ge(s_bn, 3 * l + 2)
                nc.tensor.matmul(bank(1)[:, 0:1], average, small[:, 4:5], start=True, stop=True).then_inc(s_avg, 1)

            pe.wait_ge(s_chain, CHAIN_AT_PROJ)
            nc.tensor.matmul(bank(4)[:, 0:1], first, small[:, 16:17], start=True, stop=True).then_inc(s_proj, 1)
            pe.wait_ge(s_pick, 1)
            for i in range(PAIRS):
                at_least(pe, s_u, i - 3)
                for k in range(4):
                    last = nc.tensor.matmul(bank(i % 4)[Q * k:Q * (k + 1), :], m_proj[:, :], V[:, BLK * i + 512 * k:BLK * i + 512 * (k + 1)],
                                            start=True, stop=True)
                last.then_inc(s_proj, 1)


DEPTH = 4
EMB = 64
HEADS = 8
DH = EMB // HEADS
FF = 4 * EMB
TILES = BATCH * S // P
GROUPS = 2
GT = TILES // GROUPS
GP = GT // 2
GW = GT * EMB
EXPERTS = 4
HID = 128
W_QV, W_K, W_O, W_1, W_2 = 0, 256, 384, 512, 1024
W_LN, W_B1, W_BO, W_B2, W_LAYER = 1152, 1156, 1158, 1222, 1286
E_1, E_2, E_3, E_S1, E_S2, E_S3 = 0, 1024, 1280, 1536, 1664, 1920
E_G, E_B1, E_B2, E_SB1, E_SB2, E_GB, E_B3, E_SB3, E_ALL = 1984, 1992, 1996, 1998, 1999, 2000, 2004, 2260, 2324


def token_layout(Wq, Wk, Wv, Wo, bo, ln1_g, ln1_b, W1, b1, W2, b2, ln2_g, ln2_b):
    out = np.zeros((DEPTH, P, W_LAYER), np.float32)
    for l in range(DEPTH):
        for par in range(2):
            rows = slice(EMB * par, EMB * (par + 1))
            cols = EMB * par
            out[l, rows, W_QV + cols:W_QV + cols + EMB] = Wq[l]
            out[l, rows, W_QV + P + cols:W_QV + P + cols + EMB] = Wv[l]
            out[l, rows, W_K + cols:W_K + cols + EMB] = Wk[l]
            out[l, rows, W_O + cols:W_O + cols + EMB] = Wo[l]
            out[l, rows, W_1 + FF * par:W_1 + FF * (par + 1)] = W1[l]
            for i, v in enumerate((ln1_g, ln1_b, ln2_g, ln2_b)):
                out[l, rows, W_LN + i] = v[l]
        for c in range(2):
            out[l, :, W_2 + EMB * c:W_2 + EMB * (c + 1)] = W2[l, P * c:P * (c + 1)]
            out[l, :, W_B1 + c] = b1[l, P * c:P * (c + 1)]
        out[l, :, W_BO:W_BO + EMB] = bo[l]
        out[l, :, W_B2:W_B2 + EMB] = b2[l]
    return out


def mixture_layout(sW1, sb1, sW2, sb2, sW3, sb3, eW1, eb1, eW2, eb2, eW3, eb3, gW, gb):
    out = np.zeros((P, E_ALL), np.float32)
    for par in range(2):
        rows = slice(EMB * par, EMB * (par + 1))
        for e in range(EXPERTS):
            at = E_1 + HID * (2 * e + par)
            out[rows, at:at + HID] = eW1[e]
        out[rows, E_S1 + EMB * par:E_S1 + EMB * (par + 1)] = sW1
        out[rows, E_S2 + P * par:E_S2 + P * (par + 1)] = sW2
        out[rows, E_SB1] = sb1
        out[rows, E_G + EXPERTS * par:E_G + EXPERTS * (par + 1)] = gW
        for ep in range(2):
            out[rows, E_3 + P * ep + EMB * par:E_3 + P * ep + EMB * (par + 1)] = eW3[2 * ep + par]
            out[rows, E_B2 + ep] = eb2[2 * ep + par]
    for e in range(EXPERTS):
        out[:, E_2 + EMB * e:E_2 + EMB * (e + 1)] = eW2[e]
        out[:, E_B1 + e] = eb1[e]
        out[:, E_B3 + EMB * e:E_B3 + EMB * (e + 1)] = eb3[e]
    out[:, E_S3:E_S3 + EMB] = sW3
    out[:, E_SB2] = sb2
    out[:, E_SB3:E_SB3 + EMB] = sb3
    out[:, E_GB:E_GB + EXPERTS] = gb
    return out


def token_constants():
    own = np.kron(np.eye(2 * HEADS), np.ones((DH, DH)))
    return np.concatenate([np.eye(P), own], axis=1).astype(np.float32)


def token_kernel(nc, tower_out, layers, mixture, table, out):
    f32 = mybir.dt.float32
    ALU = mybir.AluOpType
    ACT = mybir.ActivationFunctionType
    X_AXIS = mybir.AxisListType.X
    SCALE = DH ** -0.25
    G = GROUPS
    NX = TILES * EMB

    with ExitStack() as ctx:
        def sb(name, shape):
            return ctx.enter_context(nc.sbuf_tensor(name, shape, f32))

        def sem(name):
            return ctx.enter_context(nc.semaphore(name))

        u0 = sb("u0", [P, NX])
        xr = sb("xr", [P, NX])
        xb = sb("xb", [P, NX])
        cen = sb("cen", [P, NX])
        sq = sb("sq", [P, NX])
        nrm = sb("nrm", [P, NX])
        hT = sb("hT", [P, NX])
        qs = sb("qs", [P, NX])
        qe = sb("qe", [P, NX])
        ks = sb("ks", [P, NX])
        ke = sb("ke", [P, NX])
        qT = sb("qT", [P, NX])
        kt = sb("kt", [P, NX])
        vd = sb("vd", [P, 2 * NX])
        cx = sb("cx", [P, 2 * NX])
        oT = sb("oT", [P, NX])
        gl = sb("gl", [P, 4 * NX])
        wl = sb("wl", [P, 2, W_LAYER])
        wm = sb("wm", [P, E_ALL])
        cst = sb("cst", [P, 2 * P])
        st = sb("st", [P, 12, TILES])
        hst = sb("hst", [P, 4, TILES * HEADS])
        kst = sb("kst", [P, 4, TILES])
        gates = sb("gates", [P, 8, TILES * EXPERTS])
        ps = ctx.enter_context(nc.psum_tensor("tps", [P, 4096], f32))
        ident, own = cst[:, 0:P], cst[:, P:2 * P]

        def bank(g, i, n=1):
            return ps[:, 512 * (4 * g + i):512 * (4 * g + i + n)]

        def part(a, g, k=1):
            return a[:, k * GW * g:k * GW * (g + 1)]

        def stat(i, g):
            return st[:, i, GT * g:GT * (g + 1)]

        s_u = sem("s_tokens")
        s_wl = [sem("s_wl0"), sem("s_wl1")]
        s_wm = sem("s_wm")
        s_cst = sem("s_cst")
        s_vzero = sem("s_vzero")
        s_link = sem("s_link")
        s_cen = sem("s_cen")
        s_sq = sem("s_sq")
        s_var = sem("s_var")
        s_dev = sem("s_dev")
        s_nrm = sem("s_nrm")
        s_tr = sem("s_tr")
        s_hT = sem("s_hT")
        s_qkv = sem("s_qkv")
        s_vd = sem("s_vd")
        s_ks = sem("s_ks")
        s_qs = sem("s_qs")
        s_ke = sem("s_ke")
        s_qe = sem("s_qe")
        s_kn = sem("s_kn")
        s_qn = sem("s_qn")
        s_ktp = sem("s_ktp")
        s_qtp = sem("s_qtp")
        s_kt = sem("s_kt")
        s_qT = sem("s_qT")
        s_ctx = sem("s_ctx")
        s_cx = sem("s_cx")
        s_otp = sem("s_otp")
        s_oT = sem("s_oT")
        s_wo = sem("s_wo")
        s_xb = sem("s_xb")
        s_x = sem("s_x")
        s_ff = sem("s_ff")
        s_gl = sem("s_gl")
        s_ff2 = sem("s_ff2")
        s_gate = sem("s_gate")
        s_coef = sem("s_coef")
        s_m1 = sem("s_m1")
        s_m1a = sem("s_m1a")
        s_m1v = sem("s_m1v")
        s_m2 = sem("s_m2")
        s_m2a = sem("s_m2a")
        s_m2v = sem("s_m2v")
        s_m3 = sem("s_m3")
        s_m3b = sem("s_m3b")
        s_sh1 = sem("s_sh1")
        s_sh2 = sem("s_sh2")
        s_gexp = sem("s_gexp")
        s_glog = sem("s_glog")
        s_out = sem("s_done")

        h1 = sb("h1", [P, 18 * 512])
        h2 = sb("h2", [P, 12 * 512])

        def hidden_1(i):
            bias = wm[:, E_B1 + i // 4:E_B1 + i // 4 + 1] if i < 16 else wm[:, E_SB1:E_SB1 + 1]
            return h1[:, 512 * i:512 * (i + 1)], bias

        def hidden_2(i):
            bias = wm[:, E_B2 + i // 4:E_B2 + i // 4 + 1] if i < 8 else wm[:, E_SB2:E_SB2 + 1]
            return h2[:, 512 * i:512 * (i + 1)], bias

        block = ctx.enter_context(nc.Block())

        def norm_index(l, which):
            return (2 * l + which) * G

        LAST = 2 * DEPTH

        @block.sync
        def _(sp):
            sp.dma_start(cst[:, :], table).then_inc(s_cst, 16)
            u_view = u0[:, :].rearrange("p (t y) -> p t y", y=S)
            for k in range(4):
                for b2 in range(2):
                    for yh in range(2):
                        row = 4 * k + 2 * b2 + yh
                        sp.dma_start(u_view[S * b2 + 16 * k:S * b2 + 16 * (k + 1), :, yh * Q:(yh + 1) * Q],
                                     tower_out[row].rearrange("(i x y) -> x i y", i=PAIRS, x=16)).then_inc(s_u, 16)
            for l in range(DEPTH):
                if l >= 2:
                    sp.wait_ge(s_x, 2 * G * (l - 1))
                sp.dma_start(wl[:, l % 2, :], layers[l]).then_inc(s_wl[l % 2], 16)
            sp.dma_start(wm[:, :], mixture).then_inc(s_wm, 16)
            for g in range(G):
                sp.wait_ge(s_nrm, norm_index(DEPTH, 1) + g + 1)
                sp.dma_start(out[2 * GT * g:2 * GT * (g + 1)].rearrange("(t b) x y -> (b x) t y", b=2),
                             part(nrm, g).rearrange("p (t y) -> p t y", y=S)).then_inc(s_out, 16)
            sp.wait_ge(s_out, 16 * G)

        @block.gpsimd
        def _(pool):
            nc.gpsimd.memset(vd[:, :], 0.0).then_inc(s_vzero, 1)
            for l in range(DEPTH):
                pool.wait_ge(s_wl[l % 2], 16 * (l // 2 + 1))
                for which, at in enumerate((W_BO, W_B2)):
                    bias = wl[:, l % 2, at:at + EMB].unsqueeze(1).broadcast_to([P, GT, EMB])
                    for g in range(G):
                        n = norm_index(l, which)
                        if n:
                            pool.wait_ge(s_x, n - G + g + 1)
                        else:
                            pool.wait_ge(s_u, 256)
                        src = part(xr if n else u0, g)
                        nc.gpsimd.tensor_tensor(part(xb, g).rearrange("p (t e) -> p t e", e=EMB),
                                                src.rearrange("p (t e) -> p t e", e=EMB), bias, ALU.add).then_inc(s_xb, 1)

        @block.scalar
        def _(act):
            def square_root(n):
                for g in range(G):
                    act.wait_ge(s_cen, n + g + 1)
                    nc.scalar.activation(part(sq, g), part(cen, g), ACT.Square).then_inc(s_sq, 1)
                for g in range(G):
                    act.wait_ge(s_var, n + g + 1)
                    nc.scalar.activation(stat(3, g), stat(2, g), ACT.Sqrt).then_inc(s_dev, 1)

            def transposed(n, l, which):
                for g in range(G):
                    act.wait_ge(s_tr, n + g + 1)
                    w = wl[:, l % 2, W_LN + 2 * which:W_LN + 2 * which + 2]
                    nc.scalar.activation(part(hT, g), bank(g, 0), ACT.Identity, bias=w[:, 1:2],
                                         scale=w[:, 0:1]).then_inc(s_hT, 1)

            act.wait_ge(s_vzero, 1)
            for l in range(DEPTH):
                n = norm_index(l, 0)
                square_root(n)
                act.wait_ge(s_wl[l % 2], 16 * (l // 2 + 1))
                transposed(n, l, 0)
                for g in range(G):
                    act.wait_ge(s_qkv, l * G + g + 1)
                    for b in range(2):
                        rows = slice(S * b, S * (b + 1))
                        dst = part(vd, g, 2)[rows].rearrange("p (t h c) -> p t h c", h=2, c=P)[:, :, b]
                        src = bank(g, 2)[rows].rearrange("p (t c) -> p t c", c=P)
                        nc.scalar.copy(dst, src).then_inc(s_vd, 1)
                for g in range(G):
                    act.wait_ge(s_ks, l * G + g + 1)
                    nc.scalar.activation(part(ke, g), part(ks, g), ACT.Exp, scale=SCALE).then_inc(s_ke, 1)
                    act.wait_ge(s_qs, l * G + g + 1)
                    nc.scalar.activation(part(qe, g), part(qs, g), ACT.Exp, scale=SCALE).then_inc(s_qe, 1)
                for g in range(G):
                    act.wait_ge(s_qtp, l * G + g + 1)
                    nc.scalar.copy(part(qT, g), bank(g, 0)).then_inc(s_qT, 1)
                for g in range(G):
                    act.wait_ge(s_otp, l * G + g + 1)
                    nc.scalar.copy(part(oT, g), bank(g, 0)).then_inc(s_oT, 1)
                n = norm_index(l, 1)
                square_root(n)
                transposed(n, l, 1)
                for g in range(G):
                    for i in range(4):
                        act.wait_ge(s_ff, 4 * (l * G + g) + i + 1)
                        c = i % 2
                        nc.scalar.activation(part(gl, g, 4)[:, GW * i:GW * (i + 1)], bank(g, i), ACT.Gelu,
                                             bias=wl[:, l % 2, W_B1 + c:W_B1 + c + 1]).then_inc(s_gl, 1)
            n = norm_index(DEPTH, 0)
            square_root(n)
            for g in range(G):
                act.wait_ge(s_tr, n + g + 1)
                nc.scalar.copy(part(hT, g), bank(g, 0)).then_inc(s_hT, 1)
            act.wait_ge(s_glog, 1)
            nc.scalar.activation(gates[:, 1, :], gates[:, 0, :], ACT.Exp).then_inc(s_gexp, 1)
            act.wait_ge(s_wm, 16)
            for i in range(0, 18, 2):
                act.wait_ge(s_m1, i + 1)
                dst, bias = hidden_1(i)
                nc.scalar.activation(dst, ps[:, 512 * (i % 8):512 * (i % 8 + 1)], ACT.Relu, bias=bias).then_inc(s_m1a, 1)
            for i in range(0, 12, 2):
                act.wait_ge(s_m2, i + 1)
                dst, bias = hidden_2(i)
                nc.scalar.activation(dst, ps[:, 512 * ((i + 18) % 8):512 * ((i + 18) % 8 + 1)], ACT.Relu,
                                     bias=bias).then_inc(s_m2a, 1)
            act.wait_ge(s_gexp, 2)
            nc.scalar.activation(st[:, 8, :], st[:, 7, :], ACT.Exp).then_inc(s_gexp, 1)
            square_root(norm_index(DEPTH, 1))

        @block.vector
        def _(dve):
            chain = [0]

            def link(ins):
                chain[0] += 1
                ins.then_inc(s_link, 1)
                dve.wait_ge(s_link, chain[0])

            def normalise(n, src, ready):
                for g in range(G):
                    ready(g)
                    x3 = part(src, g).rearrange("p (t e) -> p t e", e=EMB)
                    link(nc.vector.reduce_sum(stat(0, g), x3, X_AXIS))
                    link(nc.vector.tensor_scalar(stat(1, g), stat(0, g), 1.0 / EMB, None, ALU.mult))
                    if n:
                        dve.wait_ge(s_nrm, n - G + g + 1)
                    nc.vector.tensor_tensor(part(cen, g).rearrange("p (t e) -> p t e", e=EMB), x3,
                                            stat(1, g).unsqueeze(2).broadcast_to([P, GT, EMB]), ALU.subtract).then_inc(s_cen, 1)
                for g in range(G):
                    dve.wait_ge(s_sq, n + g + 1)
                    link(nc.vector.reduce_sum(stat(4, g), part(sq, g).rearrange("p (t e) -> p t e", e=EMB), X_AXIS))
                    nc.vector.tensor_scalar(stat(2, g), stat(4, g), 1.0 / EMB, EPS, ALU.mult, ALU.add).then_inc(s_var, 1)
                for g in range(G):
                    dve.wait_ge(s_dev, n + g + 1)
                    dve.wait_ge(s_var, n + g + 1)
                    link(nc.vector.reciprocal(stat(5, g), stat(3, g)))
                    link(nc.vector.tensor_tensor(stat(6, g), stat(5, g), stat(5, g), ALU.mult))
                    link(nc.vector.tensor_tensor(stat(6, g), stat(6, g), stat(2, g), ALU.mult))
                    link(nc.vector.tensor_scalar(stat(6, g), stat(6, g), -0.5, 1.5, ALU.mult, ALU.add))
                    link(nc.vector.tensor_tensor(stat(5, g), stat(5, g), stat(6, g), ALU.mult))
                    nc.vector.tensor_tensor(part(nrm, g).rearrange("p (t e) -> p t e", e=EMB),
                                            part(cen, g).rearrange("p (t e) -> p t e", e=EMB),
                                            stat(5, g).unsqueeze(2).broadcast_to([P, GT, EMB]), ALU.mult).then_inc(s_nrm, 1)

            def residual(n, b, done, count):
                for g in range(G):
                    dve.wait_ge(done, count + g + 1)
                    dve.wait_ge(s_xb, n + g + 1)
                    nc.vector.tensor_tensor(part(xr, g), bank(g, b), part(xb, g), ALU.add).then_inc(s_x, 1)

            for l in range(DEPTH):
                n = norm_index(l, 0)
                if l:
                    normalise(n, xr, lambda g: dve.wait_ge(s_x, n - G + g + 1))
                else:
                    dve.wait_ge(s_u, 256)
                    normalise(0, u0, lambda g: None)
                for g in range(G):
                    dve.wait_ge(s_qkv, l * G + g + 1)
                    k3 = bank(g, 3).rearrange("p (i n) -> p i n", n=S)
                    kmax, hmax = kst[:, 0, GT * g:GT * (g + 1)], hst[:, 0, S * g:S * (g + 1)]
                    link(nc.vector.reduce_max(kmax, k3, X_AXIS))
                    nc.vector.tensor_tensor(part(ks, g).rearrange("p (i n) -> p i n", n=S), k3,
                                            kmax.unsqueeze(2).broadcast_to([P, GT, S]), ALU.subtract).then_inc(s_ks, 1)
                    q4 = bank(g, 1).rearrange("p (t h d) -> p t h d", h=2 * HEADS, d=DH)
                    hm = hmax.rearrange("p (t h) -> p t h", h=2 * HEADS)
                    link(nc.vector.reduce_max(hm, q4, X_AXIS))
                    nc.vector.tensor_tensor(part(qs, g).rearrange("p (t h d) -> p t h d", h=2 * HEADS, d=DH), q4,
                                            hm.unsqueeze(3).broadcast_to([P, GP, 2 * HEADS, DH]), ALU.subtract).then_inc(s_qs, 1)
                for g in range(G):
                    dve.wait_ge(s_ke, l * G + g + 1)
                    k3 = part(ke, g).rearrange("p (i n) -> p i n", n=S)
                    ksum, krec = kst[:, 1, GT * g:GT * (g + 1)], kst[:, 2, GT * g:GT * (g + 1)]
                    link(nc.vector.reduce_sum(ksum, k3, X_AXIS))
                    link(nc.vector.reciprocal(krec, ksum))
                    nc.vector.tensor_tensor(part(ks, g).rearrange("p (i n) -> p i n", n=S), k3,
                                            krec.unsqueeze(2).broadcast_to([P, GT, S]), ALU.mult).then_inc(s_kn, 1)
                    dve.wait_ge(s_qe, l * G + g + 1)
                    q3 = part(qe, g).rearrange("p (h d) -> p h d", d=DH)
                    hsum, hrec = hst[:, 1, S * g:S * (g + 1)], hst[:, 2, S * g:S * (g + 1)]
                    link(nc.vector.reduce_sum(hsum, q3, X_AXIS))
                    link(nc.vector.reciprocal(hrec, hsum))
                    nc.vector.tensor_tensor(part(qs, g).rearrange("p (h d) -> p h d", d=DH), q3,
                                            hrec.unsqueeze(2).broadcast_to([P, S, DH]), ALU.mult).then_inc(s_qn, 1)
                for g in range(G):
                    dve.wait_ge(s_ktp, l * G + g + 1)
                    nc.vector.tensor_copy(part(kt, g), bank(g, 3)).then_inc(s_kt, 1)
                for g in range(G):
                    dve.wait_ge(s_ctx, l * G + g + 1)
                    nc.vector.tensor_tensor(part(cx, g, 2).rearrange("p (i c) -> p i c", c=P),
                                            bank(g, 1, 2).rearrange("p (i c) -> p i c", c=P),
                                            own.unsqueeze(1).broadcast_to([P, GT, P]), ALU.mult).then_inc(s_cx, 1)
                residual(n, 3, s_wo, l * G)
                n = norm_index(l, 1)
                normalise(n, xr, lambda g: dve.wait_ge(s_x, n - G + g + 1))
                residual(n, 0, s_ff2, l * G)
            n = norm_index(DEPTH, 0)
            dve.wait_ge(s_x, n)
            link(nc.vector.tensor_tensor(xr[:, :], xr[:, :], u0[:, :], ALU.add))
            normalise(n, xr, lambda g: None)

            dve.wait_ge(s_gate, 1)
            dve.wait_ge(s_wm, 16)
            te = [P, TILES, EXPERTS]

            def gate(i):
                return gates[:, i, :].rearrange("p (t e) -> p t e", e=EXPERTS)

            def spread(i):
                return st[:, i, :].unsqueeze(2).broadcast_to(te)

            link(nc.vector.tensor_tensor(gate(2), ps[:, 0:TILES * EXPERTS].rearrange("p (t e) -> p t e", e=EXPERTS),
                                         wm[:, E_GB:E_GB + EXPERTS].unsqueeze(1).broadcast_to(te), ALU.add))
            link(nc.vector.reduce_max(st[:, 9, :], gate(2), X_AXIS))
            nc.vector.tensor_tensor(gate(0), gate(2), spread(9), ALU.subtract).then_inc(s_glog, 1)
            dve.wait_ge(s_gexp, 1)
            link(nc.vector.reduce_sum(st[:, 9, :], gate(1), X_AXIS))
            link(nc.vector.reciprocal(st[:, 10, :], st[:, 9, :]))
            link(nc.vector.tensor_tensor(gate(2), gate(1), spread(10), ALU.mult))

            def pick_first(values, best, chosen, equal, left):
                link(nc.vector.reduce_max(st[:, best, :], gate(values), X_AXIS))
                link(nc.vector.tensor_tensor(gate(equal), gate(values), spread(best), ALU.is_ge))
                link(nc.vector.memset(st[:, left, :], 1.0))
                for e in range(EXPERTS):
                    link(nc.vector.tensor_tensor(gate(chosen)[:, :, e], gate(equal)[:, :, e], st[:, left, :], ALU.mult))
                    link(nc.vector.tensor_tensor(st[:, left, :], st[:, left, :], gate(chosen)[:, :, e], ALU.subtract))

            pick_first(2, 9, 3, 4, 11)
            link(nc.vector.scalar_tensor_tensor(out=gates[:, 5, :], in0=gates[:, 3, :], scalar=-2.0, in1=gates[:, 2, :],
                                                op0=ALU.mult, op1=ALU.add))
            pick_first(5, 10, 6, 4, 11)
            nc.vector.tensor_tensor(st[:, 7, :], st[:, 10, :], st[:, 9, :], ALU.subtract).then_inc(s_gexp, 1)

            for i in range(1, 18, 2):
                dve.wait_ge(s_m1, i + 1)
                dst, bias = hidden_1(i)
                nc.vector.tensor_scalar(dst, ps[:, 512 * (i % 8):512 * (i % 8 + 1)], bias, 0.0, ALU.add, ALU.max).then_inc(s_m1v, 1)
            for i in range(1, 12, 2):
                dve.wait_ge(s_m2, i + 1)
                dst, bias = hidden_2(i)
                nc.vector.tensor_scalar(dst, ps[:, 512 * ((i + 18) % 8):512 * ((i + 18) % 8 + 1)], bias, 0.0,
                                        ALU.add, ALU.max).then_inc(s_m2v, 1)

            dve.wait_ge(s_gexp, 3)
            link(nc.vector.tensor_scalar(st[:, 9, :], st[:, 8, :], 1.0, None, ALU.add))
            link(nc.vector.reciprocal(st[:, 10, :], st[:, 9, :]))
            link(nc.vector.tensor_tensor(gate(4), gate(6), spread(8), ALU.mult))
            link(nc.vector.tensor_tensor(gate(4), gate(4), gate(3), ALU.add))
            link(nc.vector.tensor_tensor(gate(7), gate(4), spread(10), ALU.mult))

            link(nc.vector.tensor_tensor(xr[:, :].rearrange("p (t e) -> p t e", e=EMB), nrm[:, :].rearrange("p (t e) -> p t e", e=EMB),
                                         wm[:, E_SB3:E_SB3 + EMB].unsqueeze(1).broadcast_to([P, TILES, EMB]), ALU.add))
            four = [P, 2, EXPERTS, EMB]
            for t in range(TILES // 2):
                dve.wait_ge(s_m3, t + 1)
                pick = gl[:, 512 * (t % 2):512 * (t % 2 + 1)]
                p4 = pick.rearrange("p (t e c) -> p t e c", t=2, c=EMB)
                src = ps[:, 512 * (t % 4):512 * (t % 4 + 1)].rearrange("p (t e c) -> p t e c", t=2, c=EMB)
                bias = wm[:, E_B3:E_B3 + EXPERTS * EMB].rearrange("p (e c) -> p e c", c=EMB).unsqueeze(1).broadcast_to(four)
                nc.vector.tensor_tensor(p4, src, bias, ALU.add).then_inc(s_m3b, 1)
                dve.wait_ge(s_m3b, t + 1)
                coef = gate(7)[:, 2 * t:2 * t + 2, :].unsqueeze(3).broadcast_to(four)
                link(nc.vector.tensor_tensor(p4, p4, coef, ALU.mult))
                link(nc.vector.reduce_sum(sq[:, P * t:P * (t + 1)].rearrange("p (t c) -> p t c", c=EMB),
                                          pick.rearrange("p (t e c) -> p t c e", t=2, c=EMB), X_AXIS))
            dve.wait_ge(s_sh2, 2)
            link(nc.vector.tensor_tensor(xr[:, :], xr[:, :], sq[:, :], ALU.add))
            link(nc.vector.tensor_tensor(xr[:, :], xr[:, :], ps[:, 2048:2048 + NX], ALU.add))
            normalise(norm_index(DEPTH, 1), xr, lambda g: None)

        @block.tensor
        def _(pe):
            def transposes(n):
                for g in range(G):
                    pe.wait_ge(s_nrm, n + g + 1)
                    for t in range(GP):
                        last = nc.tensor.transpose(bank(g, 0)[:, P * t:P * (t + 1)], part(nrm, g)[:, P * t:P * (t + 1)], ident)
                    last.then_inc(s_tr, 1)

            pe.wait_ge(s_cst, 16)
            for l in range(DEPTH):
                w = wl[:, l % 2, :]
                n = norm_index(l, 0)
                transposes(n)
                pe.wait_ge(s_wl[l % 2], 16 * (l // 2 + 1))
                for g in range(G):
                    pe.wait_ge(s_hT, n + g + 1)
                    h = part(hT, g)
                    nc.tensor.matmul(bank(g, 3), w[:, W_K:W_K + P], h, start=True, stop=True)
                    for t in range(GP):
                        for i in range(2):
                            last = nc.tensor.matmul(bank(g, 1 + i)[:, P * t:P * (t + 1)], h[:, P * t:P * (t + 1)],
                                                    w[:, W_QV + P * i:W_QV + P * (i + 1)], start=True, stop=True)
                    last.then_inc(s_qkv, 1)
                for g in range(G):
                    pe.wait_ge(s_kn, l * G + g + 1)
                    for t in range(GP):
                        last = nc.tensor.transpose(bank(g, 3)[:, P * t:P * (t + 1)], part(ks, g)[:, P * t:P * (t + 1)], ident)
                    last.then_inc(s_ktp, 1)
                    pe.wait_ge(s_qn, l * G + g + 1)
                    for t in range(GP):
                        last = nc.tensor.transpose(bank(g, 0)[:, P * t:P * (t + 1)], part(qs, g)[:, P * t:P * (t + 1)], ident)
                    last.then_inc(s_qtp, 1)
                for g in range(G):
                    pe.wait_ge(s_kt, l * G + g + 1)
                    pe.wait_ge(s_vd, 2 * (l * G + g + 1))
                    for t in range(GP):
                        last = nc.tensor.matmul(bank(g, 1, 2)[:, 2 * P * t:2 * P * (t + 1)], part(kt, g)[:, P * t:P * (t + 1)],
                                                part(vd, g, 2)[:, 2 * P * t:2 * P * (t + 1)], start=True, stop=True)
                    last.then_inc(s_ctx, 1)
                for g in range(G):
                    pe.wait_ge(s_cx, l * G + g + 1)
                    pe.wait_ge(s_qT, l * G + g + 1)
                    for i in range(GT):
                        last = nc.tensor.matmul(bank(g, 0)[:, S * i:S * (i + 1)], part(cx, g, 2)[:, P * i:P * (i + 1)],
                                                part(qT, g)[:, S * i:S * (i + 1)], start=True, stop=True)
                    last.then_inc(s_otp, 1)
                for g in range(G):
                    pe.wait_ge(s_oT, l * G + g + 1)
                    for t in range(GP):
                        last = nc.tensor.matmul(bank(g, 3)[:, P * t:P * (t + 1)], part(oT, g)[:, P * t:P * (t + 1)],
                                                w[:, W_O:W_O + P], start=True, stop=True)
                    last.then_inc(s_wo, 1)
                n = norm_index(l, 1)
                transposes(n)
                for g in range(G):
                    pe.wait_ge(s_hT, n + g + 1)
                    for i in range(4):
                        at = W_1 + P * i
                        nc.tensor.matmul(bank(g, i), w[:, at:at + P], part(hT, g), start=True, stop=True).then_inc(s_ff, 1)
                for g in range(G):
                    pe.wait_ge(s_gl, 4 * (l * G + g + 1))
                    for t in range(GT):
                        for c in range(2):
                            at = GW * (2 * (t % 2) + c) + P * (t // 2)
                            last = nc.tensor.matmul(bank(g, 0)[:, EMB * t:EMB * (t + 1)], part(gl, g, 4)[:, at:at + P],
                                                    w[:, W_2 + EMB * c:W_2 + EMB * (c + 1)], start=c == 0, stop=c == 1)
                    last.then_inc(s_ff2, 1)

            transposes(norm_index(DEPTH, 0))
            pe.wait_ge(s_wm, 16)
            pe.wait_ge(s_hT, norm_index(DEPTH, 1))
            for t in range(TILES // 2):
                last = nc.tensor.matmul(ps[:, 2 * EXPERTS * t:2 * EXPERTS * (t + 1)], hT[:, P * t:P * (t + 1)],
                                        wm[:, E_G:E_G + 2 * EXPERTS], start=True, stop=True)
            last.then_inc(s_gate, 1)
            pe.wait_ge(s_glog, 1)
            for i in range(18):
                if i >= 8:
                    pe.wait_ge(s_m1v if i % 2 else s_m1a, (i - 8) // 2 + 1)
                w = wm[:, E_1 + HID * (i // 2):E_1 + HID * (i // 2 + 1)] if i < 16 else wm[:, E_S1:E_S1 + P]
                nc.tensor.matmul(ps[:, 512 * (i % 8):512 * (i % 8 + 1)], w, part(hT, i % 2), start=True, stop=True).then_inc(s_m1, 1)
            pe.wait_ge(s_m1v, 9)
            pe.wait_ge(s_m1a, 9)
            for i in range(12):
                if i >= 8:
                    pe.wait_ge(s_m2v if i % 2 else s_m2a, (i - 8) // 2 + 1)
                at = (i + 18) % 8
                if i < 8:
                    for e2 in range(2):
                        e = 2 * (i // 4) + e2
                        src = 4 * e + i % 4
                        last = nc.tensor.matmul(ps[EMB * e2:EMB * (e2 + 1), 512 * at:512 * (at + 1)], wm[:, E_2 + EMB * e:E_2 + EMB * (e + 1)],
                                                h1[:, 512 * src:512 * (src + 1)], start=True, stop=True)
                else:
                    par = (i - 8) // 2
                    last = nc.tensor.matmul(ps[:, 512 * at:512 * (at + 1)], wm[:, E_S2 + P * par:E_S2 + P * (par + 1)],
                                            h1[:, 512 * (16 + i % 2):512 * (17 + i % 2)], start=True, stop=True)
                last.then_inc(s_m2, 1)
            pe.wait_ge(s_m2v, 6)
            pe.wait_ge(s_m2a, 6)

            def place(t):
                return t % 2, t // GT, P * ((t % GT) // 2)

            for half in range(2):
                for t in range(GT * half, GT * (half + 1)):
                    par, g, col = place(t)
                    at = 512 * (8 + 2 * par + g) + col
                    last = nc.tensor.matmul(ps[:, 2048 + EMB * t:2048 + EMB * (t + 1)], h2[:, at:at + P],
                                            wm[:, E_S3:E_S3 + EMB], start=True, stop=True)
                last.then_inc(s_sh2, 1)
            for t in range(TILES):
                par, g, col = place(t)
                if t % 2 == 0 and t >= 8:
                    pe.wait_ge(s_m3b, (t - 8) // 2 + 1)
                for ep in range(2):
                    at = 512 * (4 * ep + 2 * par + g) + col
                    dst = 512 * ((t // 2) % 4) + 256 * (t % 2) + P * ep
                    last = nc.tensor.matmul(ps[:, dst:dst + P], h2[:, at:at + P], wm[:, E_3 + P * ep:E_3 + P * (ep + 1)],
                                            start=True, stop=True)
                if t % 2:
                    last.then_inc(s_m3, 1)


_TOWER = ["p_w", "p_b", "fw1", "fw2", "w_w", "w_b", "bn_g", "bn_b", "q_w", "q_b"]
_ATTN = ["Wq", "Wk", "Wv", "Wo", "bo", "ln1_g", "ln1_b", "W1", "b1", "W2", "b2", "ln2_g", "ln2_b"]
_FFN = ["sW1", "sb1", "sW2", "sb2", "sW3", "sb3", "eW1", "eb1", "eW2", "eb2", "eW3", "eb3", "gW", "gb"]


def kernel(**inputs):
    import numpy as _np
    import concourse.bacc as _bacc
    from concourse import mybir as _mybir
    from concourse.bass_utils import run_bass_kernel_spmd as _run

    def given(prefix, names):
        return {n: _np.asarray(inputs[prefix + n]) for n in names}

    pixels, weights, modes = tower_layout(_np.asarray(inputs["x"]), **given("L0_tok_", _TOWER))
    table, grid = constants()
    arrays = {
        "pixels": pixels, "weights": weights, "modes": modes, "table": table, "grid": grid,
        "layers": token_layout(**given("L0_attn_", _ATTN)),
        "mixture": mixture_layout(**given("L0_ffn_", _FFN)),
        "token_table": token_constants(),
    }
    arrays = {f"in_{k}": _np.ascontiguousarray(v) for k, v in arrays.items()}
    nc = _bacc.Bacc("TRN2", target_bir_lowering=False, num_devices=1)
    f32 = _mybir.dt.float32
    a = {k: nc.dram_tensor(k, v.shape, f32, kind="ExternalInput").ap() for k, v in arrays.items()}
    out = nc.dram_tensor("out_dram", (BATCH, S, S), f32, kind="ExternalOutput").ap()
    scratch = nc.dram_tensor("tower_out", (16, PAIRS * 512), f32, kind="Internal").ap()
    tower_kernel(nc, a["in_pixels"], a["in_weights"], a["in_modes"], a["in_table"], a["in_grid"], scratch)
    token_kernel(nc, scratch, a["in_layers"], a["in_mixture"], a["in_token_table"], out)
    r = _run(nc, [arrays], core_ids=[0])
    return r.results[0]["out_dram"]
```

```python
import numpy as np
import concourse.bass as bass
from concourse import mybir
from contextlib import ExitStack

LAYERS = 4
BATCH = 32
S = 64
CH = 32
MODES = 12
Q = 32
P = 128
PAIRS = BATCH // 2
KXJ = 6
EPS = 1e-5


def constants():
    two_pi = 2.0 * np.pi / S
    y = np.arange(S)
    ky = np.arange(MODES)
    cy = np.cos(two_pi * np.outer(y, ky))
    sy = np.sin(two_pi * np.outer(y, ky))
    fwd_y = np.zeros((2, S, 2, Q))
    for b in range(2):
        fwd_y[b, :, b, 0:MODES] = cy
        fwd_y[b, :, b, MODES:2 * MODES] = -sy
    freq = np.array([[KXJ * j + k if j < 2 else S - MODES + KXJ * (j - 2) + k for k in range(KXJ)]
                     for j in range(4)])
    x = np.arange(S)
    cx = np.cos(two_pi * x[:, None, None] * freq)
    sx = np.sin(two_pi * x[:, None, None] * freq)
    fwd_x = np.zeros((2, 2, 2, Q, 4, Q))
    inv_x = np.zeros((2, 4, Q, 2, 2, Q))
    for xh in range(2):
        c, s = cx[xh * Q:(xh + 1) * Q], sx[xh * Q:(xh + 1) * Q]
        for j in range(4):
            for k in range(KXJ):
                for b in range(2):
                    at = b * MODES + 2 * k
                    re, im = 2 * (j // 2), 2 * (j // 2) + 1
                    col = 2 * (KXJ * (j % 2) + k) + b
                    fwd_x[0, xh, b, :, re, col] = c[:, j, k]
                    fwd_x[0, xh, b, :, im, col] = -s[:, j, k]
                    fwd_x[1, xh, b, :, re, col] = s[:, j, k]
                    fwd_x[1, xh, b, :, im, col] = c[:, j, k]
                    inv_x[b, j, at, xh, 0] = c[:, j, k]
                    inv_x[b, j, at, xh, 1] = s[:, j, k]
                    inv_x[b, j, at + 1, xh, 0] = -s[:, j, k]
                    inv_x[b, j, at + 1, xh, 1] = c[:, j, k]
    weight = np.where(ky == 0, 1.0, 2.0) / (S * S)
    inv_y = np.zeros((2, 2, 2, Q, 2, S))
    for xh in range(2):
        for b in range(2):
            rows = slice(b * MODES, (b + 1) * MODES)
            inv_y[xh, xh, 0, rows, b] = (weight * cy).T
            inv_y[xh, xh, 1, rows, b] = -(weight * sy).T
    average = np.tile(np.eye(CH), (4, 4)) / 4.0
    first = np.zeros((P, P))
    first[0:CH] = 1.0
    pick = np.zeros((P, Q))
    for q in range(4):
        pick[q * Q:(q + 1) * Q, q] = 1.0
    table = np.concatenate([
        fwd_y.reshape(P, 2 * Q),
        fwd_x.reshape(2, P, P).transpose(1, 0, 2).reshape(P, 2 * P),
        inv_x.reshape(2, P, P).transpose(1, 0, 2).reshape(P, 2 * P),
        inv_y.reshape(2, P, P).transpose(1, 0, 2).reshape(P, 2 * P),
        average, first, pick], axis=1).astype(np.float32)
    grid = np.zeros((4, Q, S, Q), np.float32)
    line = np.linspace(0.0, 1.0, S, dtype=np.float32)
    for q in range(4):
        grid[q, 1] = line[:, None]
        grid[q, 2] = line[None, (q % 2) * Q:(q % 2) * Q + Q]
        grid[q, 3] = 1.0
    lines = line.astype(np.float64)
    wave_x = np.exp(-1j * two_pi * np.outer(freq.reshape(2, 2 * KXJ), x)).reshape(2, 2 * KXJ, S)
    wave_y = np.exp(-1j * two_pi * np.outer(ky, y))
    one = np.ones(S)
    grid_spec = np.zeros((2, 2, 2 * KXJ, 2, 3, MODES))
    for f, (fx, fy) in enumerate(((lines, one), (one, lines), (one, one))):
        both = np.einsum("jk,m->jkm", wave_x @ fx, wave_y @ fy)
        for b in range(2):
            grid_spec[:, 0, :, b, f] = both.real
            grid_spec[:, 1, :, b, f] = both.imag
    spectra = np.zeros((2, 2, Q, 3 * MODES), np.float32)
    spectra[:, :, 0:4 * KXJ] = grid_spec.reshape(2, 2, 4 * KXJ, 3 * MODES)
    return table, grid.reshape(P, S * Q), spectra.reshape(P, 3 * MODES)


def tower_layout(x, p_w, p_b, fw1, fw2, w_w, w_b, bn_g, bn_b, q_w, q_b):
    pixels = x.reshape(PAIRS, 2, S, 2, Q).transpose(1, 3, 0, 2, 4).reshape(4, PAIRS * S * Q)
    turned = x.reshape(PAIRS, 2, S, S).transpose(1, 3, 0, 2).reshape(P, PAIRS * S)
    lift = np.zeros((4, CH, 4, Q), np.float32)
    conv = np.zeros((4, CH, LAYERS, 4, CH), np.float32)
    for q in range(4):
        lift[q, :, q, 0:3] = p_w.T
        lift[q, :, q, 3] = p_b
        conv[q, :, :, q] = w_w.transpose(1, 0, 2)
    params = np.concatenate([w_b.T, bn_g.T, bn_b.T, q_w, np.broadcast_to(q_b, (CH, 1))], axis=1)
    parts = np.stack([fw1, fw2]).transpose(1, 5, 0, 2, 4, 6, 3)
    modes = np.stack([parts, parts[..., ::-1, :]], axis=3).reshape(LAYERS * MODES, P, 2 * MODES * CH)
    weights = np.concatenate([lift.reshape(P, P), conv.reshape(P, LAYERS * P), np.tile(params, (4, 1))], axis=1)
    lift_rows = np.tile(np.concatenate([p_w.ravel(), p_b])[None], (P, 1))
    return [np.ascontiguousarray(a) for a in (pixels, turned, weights, lift_rows, modes)]


def tower_kernel(nc, pixels, turned, weights, lift_rows, modes, table, grid, grid_spectra, tower_out):
    f32 = mybir.dt.float32
    ALU = mybir.AluOpType
    ACT = mybir.ActivationFunctionType
    L = LAYERS
    HALF = (S // 2) * Q
    RBUF = 4
    BLK = 2 * HALF
    HB = Q * CH
    YR = MODES * CH
    OB = S // 2

    with ExitStack() as ctx:
        def sb(name, shape):
            return ctx.enter_context(nc.sbuf_tensor(name, shape, f32))

        def sem(name):
            return ctx.enter_context(nc.semaphore(name))

        V = sb("V", [P, PAIRS * BLK])
        spec = sb("spec", [P, MODES, PAIRS * CH])
        r_ky = sb("r_ky", [P, RBUF, MODES, 2, CH])
        arena = sb("arena", [P, 8 * HB])
        tab = sb("tab", [P, 1120])
        m_proj = sb("m_proj", [P, Q])
        wts = sb("wts", [P, P + L * P + 3 * L + 2])
        sums = sb("sums", [P, 2 * PAIRS])
        squares = sb("squares", [P, 2 * PAIRS])
        small = sb("small", [P, 24])
        ps = ctx.enter_context(nc.psum_tensor("ps", [P, 4096], f32))

        fwd_y = tab[:, 0:64]
        fwd_x = [tab[:, 64 + P * i:64 + P * (i + 1)] for i in range(2)]
        inv_x = [tab[:, 320 + P * i:320 + P * (i + 1)] for i in range(2)]
        inv_y = [tab[:, 576 + P * i:576 + P * (i + 1)] for i in range(2)]
        average = tab[:, 832:960]
        first = tab[:, 960:1088]
        pick = tab[:, 1088:1120]
        A = [arena[:, HB * i:HB * (i + 1)] for i in range(8)]
        f_act, f_tr, f_yt = A[0:2], A[2:4], A[4]
        m_in = [A[5][:, 512 * i:512 * (i + 1)] for i in range(2)]
        m_out = A[2:4]
        b_act, b_gs, b_gt, b_x1, b_sq = A[0:2], A[2], (A[3], A[6]), A[4:6], A[7]
        lift_w = wts[:, 0:P]
        room = V[:, BLK * (PAIRS - 2):]
        l_turned, l_rows, l_grid = room[:, 0:1024], room[:, 1024:1152], room[:, 1152:1152 + 3 * MODES]
        l_yt, l_spec, l_fixed, l_term = room[:, 1536:2048], room[:, 2048:2240], room[:, 2304:2688], room[:, 3072:3456]
        conv_w = [wts[:, P * (l + 1):P * (l + 2)] for l in range(L)]
        at = P * (L + 1)
        w_bias, bn_gain, bn_bias = ([wts[:, at + L * k + l:at + L * k + l + 1] for l in range(L)] for k in range(3))
        q_gain, q_bias = wts[:, at + 3 * L:at + 3 * L + 1], wts[:, at + 3 * L + 1:at + 3 * L + 2]
        flat = spec[:, :, :].rearrange("p k n -> p (k n)")
        feat = [flat[:, BLK * i:BLK * (i + 1)] for i in range(2)]

        def bank(i, n=1):
            return ps[:, 512 * i:512 * (i + n)]

        s_const = sem("s_const")
        s_feat = [sem("s_feat0"), sem("s_feat1")]
        s_lift = sem("s_lift")
        s_lyt = sem("s_lyt")
        s_lspec = sem("s_lspec")
        s_fact = sem("s_fact")
        s_ftr = sem("s_ftr")
        s_fy = sem("s_fy")
        s_fyt = sem("s_fyt")
        s_fx = sem("s_fx")
        s_spec = sem("s_spec")
        s_rload = [sem(f"s_rload{i}") for i in range(RBUF)]
        s_rky = sem("s_rky")
        s_min = sem("s_min")
        s_mix = sem("s_mix")
        s_mout = sem("s_mout")
        s_msp = sem("s_msp")
        s_gx = sem("s_gx")
        s_gs = sem("s_gs")
        s_gt = sem("s_gt")
        s_bact = sem("s_bact")
        s_iy = sem("s_iy")
        s_x1 = sem("s_x1")
        s_conv = sem("s_conv")
        s_v = sem("s_v")
        s_squares = sem("s_squares")
        s_pivot = sem("s_pivot")
        s_avg = sem("s_avg")
        s_bn = sem("s_bn")
        s_sqrt = sem("s_sqrt")
        s_norm = sem("s_norm")
        s_chain = sem("s_chain")
        s_out = sem("s_out")
        s_pads = sem("s_pads")
        s_pick = sem("s_pick")
        s_proj = sem("s_proj")
        s_u = sem("s_u")

        def at_least(eng, s, n):
            if not isinstance(n, int) or n > 0:
                eng.wait_ge(s, n)

        block = ctx.enter_context(nc.Block())

        CHAIN_AT_PROJ = 14 * L + 2 + 5 + 2 * MODES

        @block.sync
        def _(sp):
            sp.dma_start(wts[:, :], weights).then_inc(s_const, 16)
            sp.dma_start(tab[:, :], table).then_inc(s_const, 16)
            sp.dma_start(l_turned, turned).then_inc(s_const, 16)
            sp.dma_start(l_rows, lift_rows).then_inc(s_const, 16)
            sp.dma_start(l_grid, grid_spectra).then_inc(s_const, 16)

            def load_pixels(n, h):
                sp.dma_start(b_act[h][0:P:Q, :], pixels[:, bass.ds(BLK * n + HALF * h, HALF)]).then_inc(s_feat[h], 16)

            def load_modes(n):
                if n >= RBUF:
                    sp.wait_ge(s_mix, n - RBUF + 1)
                sp.dma_start(r_ky[:, n % RBUF].rearrange("p k s o -> p (k s o)"), modes[n]).then_inc(s_rload[n % RBUF], 16)

            for n in range(RBUF):
                load_modes(n)
            for h in range(2):
                sp.dma_start(b_act[h], grid[:, HALF * h:HALF * (h + 1)]).then_inc(s_feat[h], 16)
            for h in range(2):
                sp.wait_ge(s_feat[h], 16)
                load_pixels(0, h)
            for n in range(RBUF, MODES):
                load_modes(n)
            with sp.Fori(1, PAIRS) as n:
                for h in range(2):
                    sp.wait_ge(s_conv, 2 * n + h - 1)
                    load_pixels(n, h)
            for n in range(MODES, L * MODES):
                load_modes(n)
            sp.wait_ge(s_u, PAIRS)
            for k in range(4):
                src = V[Q * k:Q * k + 4, :].rearrange("p (i n) -> p i n", i=PAIRS)[:, :, 0:512]
                sp.dma_start(tower_out[4 * k:4 * k + 4, :].rearrange("q (i n) -> q i n", i=PAIRS), src).then_inc(s_out, 16)
            sp.wait_ge(s_out, 64)

        @block.gpsimd
        def _(pool):
            for n in range(L * MODES):
                pool.wait_ge(s_rload[n % RBUF], 16 * (n // RBUF + 1))
                for jj in range(2):
                    im = r_ky[64 * jj + Q:64 * (jj + 1), n % RBUF, :, 0, :]
                    nc.gpsimd.tensor_scalar(im, im, -1.0, 0.0, ALU.mult, ALU.add).then_inc(s_rky, 1)

        @block.scalar
        def _(act):
            act.wait_ge(s_lift, 3)
            nc.scalar.copy(l_spec, bank(1)[:, 0:MODES * PAIRS]).then_inc(s_lspec, 1)
            for l in range(L):
                scale, bias = small[:, 0:1], small[:, 1:2]
                if l:
                    act.wait_ge(s_norm, l)

                def f_activate(n, par):
                    for h in range(2):
                        at_least(act, s_ftr, 2 * n + h - 1 + 2 * PAIRS * (l - 1))
                        nc.scalar.activation(f_act[h], V[:, bass.ds(n * BLK + h * HALF, HALF)], ACT.Relu,
                                             bias=bias, scale=scale).then_inc(s_fact, 1)

                def f_store(n, par):
                    act.wait_ge(s_fx, n + 1 + PAIRS * (l - 1))
                    nc.scalar.copy(spec[:, :, bass.ds(n * CH, CH)],
                                   bank(4 + par)[:, 0:YR].rearrange("p (k c) -> p k c", c=CH)).then_inc(s_spec, 1)

                if l:
                    f_activate(0, 0)
                    f_activate(1, 1)
                    with act.Fori(1, PAIRS // 2) as it:
                        for par in range(2):
                            f_activate(2 * it + par, par)
                            f_store(2 * it + par - 2, par)
                    f_store(PAIRS - 2, 0)
                    f_store(PAIRS - 1, 1)

                act.wait_ge(s_pads, l + 1)
                for ky in range(MODES):
                    n = l * MODES + ky
                    act.wait_ge(s_mix, n + 1)
                    at_least(act, s_msp, n // 2 - 1)
                    for j in range(4):
                        rows = slice(Q * j, Q * (j + 1))
                        out = m_out[(n // 2) % 2][rows].rearrange("p (o s) -> p s o", s=Q)[:, (ky % 2) * MODES:(ky % 2 + 1) * MODES, :]
                        nc.scalar.copy(out, ps[rows, 512 * (4 * (n % 2) + j):512 * (4 * (n % 2) + j) + YR]
                                       .rearrange("p (s o) -> p s o", o=CH)).then_inc(s_mout, 1)

                act.wait_ge(s_msp, (MODES // 2) * (l + 1))

                def b_activate(n, par, h):
                    if l == 0:
                        return
                    act.wait_ge(s_conv, 2 * n + h - 1 + 2 * PAIRS * l)
                    nc.scalar.activation(b_act[h], V[:, bass.ds(n * BLK + h * HALF, HALF)], ACT.Relu,
                                         bias=bias, scale=scale).then_inc(s_bact, 1)

                def b_stage(n, par):
                    act.wait_ge(s_gx, n + 1 + PAIRS * l)
                    at_least(act, s_gt, n + PAIRS * l)
                    for p in range(2):
                        out = b_gs.rearrange("p (o s) -> p s o", s=Q)[:, 0:2 * MODES, :] \
                            .rearrange("p (b k e) o -> p e k b o", b=2, e=2)[:, p]
                        nc.scalar.copy(out, bank(p)[:, 0:YR].rearrange("p (k b o) -> p k b o", b=2, o=CH)).then_inc(s_gs, 1)

                def b_square(n, h):
                    act.wait_ge(s_v, 2 * n + h + 1 + 2 * PAIRS * l)
                    at_least(act, s_squares, 2 * n + h + 2 * PAIRS * l)
                    nc.scalar.activation(b_sq, V[:, bass.ds(n * BLK + h * HALF, HALF)], ACT.Square, bias=small[:, 8:9],
                                         accum_out=squares[:, bass.ds(2 * n + h, 1)]).then_inc(s_squares, 1)

                b_stage(0, 0)
                b_activate(0, 0, 0)
                b_activate(0, 0, 1)
                b_stage(1, 1)
                b_activate(1, 1, 0)
                act.wait_ge(s_pivot, l + 1)
                b_square(0, 0)
                b_activate(1, 1, 1)
                with act.Fori(0, PAIRS // 2 - 1) as it:
                    for par in range(2):
                        n = 2 * it + par
                        b_stage(n + 2, par)
                        b_square(n, 1)
                        b_activate(n + 2, par, 0)
                        b_square(n + 1, 0)
                        b_activate(n + 2, par, 1)
                b_square(PAIRS - 2, 1)
                b_square(PAIRS - 1, 0)
                b_square(PAIRS - 1, 1)
                act.wait_ge(s_bn, 3 * l + 3)
                nc.scalar.activation(small[:, 10:11], small[:, 9:10], ACT.Sqrt).then_inc(s_sqrt, 1)

            act.wait_ge(s_pick, 2)
            for i in range(PAIRS):
                act.wait_ge(s_proj, i + 2)
                nc.scalar.activation(V[:, BLK * i:BLK * i + 512], bank(i % 4), ACT.Identity,
                                     bias=small[:, 14:15], scale=1.0).then_inc(s_u, 1)

        @block.vector
        def _(dve):
            chain = [0]

            def link(ins):
                chain[0] += 1
                ins.then_inc(s_chain, 1)
                dve.wait_ge(s_chain, chain[0])

            dve.wait_ge(s_const, 80)
            dve.wait_ge(s_lift, 2)
            nc.vector.transpose(l_yt.rearrange("p (k i) -> p i k", i=PAIRS),
                                bank(0).rearrange("p (i x) -> p i x", x=Q)).then_inc(s_lyt, 1)
            wide = [P, MODES, CH]

            def lift_row(f, shape):
                return l_rows[:, CH * f:CH * (f + 1)].unsqueeze(1).broadcast_to(shape)

            fixed, term = (t.rearrange("p (k c) -> p k c", c=CH) for t in (l_fixed, l_term))
            for f in range(3):
                link(nc.vector.tensor_tensor(term if f else fixed, lift_row(f + 1, wide),
                                             l_grid[:, MODES * f:MODES * (f + 1)].unsqueeze(2).broadcast_to(wide), ALU.mult))
                if f:
                    link(nc.vector.tensor_tensor(fixed, fixed, term, ALU.add))
            dve.wait_ge(s_lift, 4)
            nc.vector.tensor_copy(lift_w, bank(2)[:, 0:P]).then_inc(s_lyt, 1)
            for l in range(L):
                def f_transpose(n, par):
                    for h in range(2):
                        dve.wait_ge(s_fact, 2 * n + h + 1 + 2 * PAIRS * (l - 1))
                        at_least(dve, s_fy, 2 * n + h - 1 + 2 * PAIRS * (l - 1))
                        nc.vector.transpose(f_tr[h], f_act[h]).then_inc(s_ftr, 1)

                def f_spectra(n, par):
                    dve.wait_ge(s_fy, 2 * n + 2 + 2 * PAIRS * (l - 1))
                    at_least(dve, s_fx, n + PAIRS * (l - 1))
                    nc.vector.transpose(f_yt.rearrange("p (k c) -> p c k", c=CH),
                                        bank(2 * par, 2).rearrange("p (x c) -> p c x", c=CH)).then_inc(s_fyt, 1)

                if l:
                    f_transpose(0, 0)
                    f_transpose(1, 1)
                    f_spectra(0, 0)
                    with dve.Fori(1, PAIRS // 2) as it:
                        for par in range(2):
                            f_transpose(2 * it + par, par)
                            f_spectra(2 * it + par - 1, 1 - par)
                    f_spectra(PAIRS - 1, 1)

                for a in m_out:
                    pads = nc.vector.memset(a.rearrange("p (o s) -> p o s", s=Q)[:, :, 2 * MODES:Q], 0.0)
                pads.then_inc(s_pads, 1)

                def mix_in(ky):
                    n = l * MODES + ky
                    if l == 0:
                        grid3 = spec[:, ky, :].rearrange("p (i c) -> p i c", c=CH)
                        three = [P, PAIRS, CH]
                        link(nc.vector.tensor_tensor(grid3, lift_row(0, three),
                                                     l_spec[:, PAIRS * ky:PAIRS * (ky + 1)].unsqueeze(2).broadcast_to(three),
                                                     ALU.mult))
                        link(nc.vector.tensor_tensor(grid3, grid3, l_fixed[:, CH * ky:CH * (ky + 1)].unsqueeze(1)
                                                     .broadcast_to(three), ALU.add))
                    at_least(dve, s_mix, n - 1)
                    nc.vector.transpose(m_in[n % 2].rearrange("p (s i) -> p i s", i=PAIRS), spec[:, ky, :]).then_inc(s_min, 1)

                if l:
                    dve.wait_ge(s_spec, PAIRS * l)
                else:
                    dve.wait_ge(s_lspec, 1)
                mix_in(0)
                mix_in(1)
                for ky in range(MODES):
                    if ky + 2 < MODES:
                        mix_in(ky + 2)
                    if ky % 2:
                        n = l * MODES + ky
                        dve.wait_ge(s_mout, 4 * (n + 1))
                        out = spec[:, ky - 1:ky + 1, :].rearrange("p k n -> p (k n)").rearrange("p (b o) -> p o b", o=CH)
                        nc.vector.transpose(out, m_out[(n // 2) % 2]).then_inc(s_msp, 1)

                def g_transpose(n, par):
                    dve.wait_ge(s_gs, 2 * n + 2 + 2 * PAIRS * l)
                    at_least(dve, s_iy, 2 * n - 2 + 2 * PAIRS * l)
                    nc.vector.transpose(b_gt[par].rearrange("p (x o) -> p o x", o=CH), b_gs).then_inc(s_gt, 1)

                def combine(n, h):
                    half = 2 * n + h + 2 * PAIRS * l
                    dve.wait_ge(s_iy, half + 1)
                    nc.vector.transpose(b_x1[h], bank(2, 2)).then_inc(s_x1, 1)
                    dve.wait_ge(s_conv, half + 1)
                    dve.wait_ge(s_x1, half + 1)
                    nc.vector.scalar_tensor_tensor(out=V[:, bass.ds(n * BLK + h * HALF, HALF)], in0=bank(4 + 2 * h, 2),
                                                   scalar=w_bias[l], in1=b_x1[h], op0=ALU.add, op1=ALU.add,
                                                   accum_out=sums[:, bass.ds(2 * n + h, 1)]).then_inc(s_v, 1)

                g_transpose(0, 0)
                combine(0, 0)
                dve.wait_ge(s_v, 2 * PAIRS * l + 1)
                nc.vector.tensor_scalar(small[:, 8:9], sums[:, 0:1], -1.0 / HALF, None, ALU.mult).then_inc(s_pivot, 1)
                g_transpose(1, 1)
                combine(0, 1)
                with dve.Fori(1, PAIRS // 2) as it:
                    for par in range(2):
                        n = 2 * it + par - 1
                        combine(n, 0)
                        g_transpose(n + 1, par)
                        combine(n, 1)
                combine(PAIRS - 1, 0)
                combine(PAIRS - 1, 1)

                dve.wait_ge(s_v, 2 * PAIRS * (l + 1))
                dve.wait_ge(s_pivot, l + 1)
                link(nc.vector.reduce_sum(small[:, 17:18], sums[:, :], mybir.AxisListType.X))
                link(nc.vector.tensor_scalar(small[:, 2:3], small[:, 17:18], 1.0 / (PAIRS * BLK), None, ALU.mult))
                link(nc.vector.tensor_scalar(small[:, 18:19], small[:, 2:3], small[:, 8:9], None, ALU.add))
                link(nc.vector.tensor_tensor(small[:, 19:20], small[:, 18:19], small[:, 18:19], ALU.mult))
                dve.wait_ge(s_squares, 2 * PAIRS * (l + 1))
                link(nc.vector.reduce_sum(small[:, 17:18], squares[:, :], mybir.AxisListType.X))
                nc.vector.scalar_tensor_tensor(out=small[:, 3:4], in0=small[:, 17:18], scalar=1.0 / (PAIRS * BLK),
                                               in1=small[:, 19:20], op0=ALU.mult, op1=ALU.subtract).then_inc(s_bn, 1)
                dve.wait_ge(s_avg, 2 * l + 1)
                dve.wait_ge(s_bn, 3 * l + 1)
                link(nc.vector.tensor_copy(small[:, 5:7], bank(0)[:, 0:2]))
                link(nc.vector.tensor_tensor(small[:, 7:8], small[:, 2:3], small[:, 5:6], ALU.subtract))
                nc.vector.tensor_tensor(small[:, 4:5], small[:, 7:8], small[:, 7:8], ALU.mult).then_inc(s_bn, 1)
                dve.wait_ge(s_avg, 2 * l + 2)
                nc.vector.tensor_scalar(small[:, 9:10], bank(1)[:, 0:1], small[:, 6:7], EPS, ALU.add, ALU.add).then_inc(s_bn, 1)
                dve.wait_ge(s_bn, 3 * l + 3)
                dve.wait_ge(s_sqrt, l + 1)
                link(nc.vector.reciprocal(small[:, 11:12], small[:, 10:11]))
                link(nc.vector.tensor_tensor(small[:, 12:13], small[:, 11:12], small[:, 11:12], ALU.mult))
                link(nc.vector.tensor_tensor(small[:, 13:14], small[:, 12:13], small[:, 9:10], ALU.mult))
                link(nc.vector.tensor_scalar(small[:, 12:13], small[:, 13:14], -0.5, 1.5, ALU.mult, ALU.add))
                link(nc.vector.tensor_tensor(small[:, 13:14], small[:, 12:13], small[:, 11:12], ALU.mult))
                link(nc.vector.tensor_tensor(small[:, 0:1], small[:, 13:14], bn_gain[l], ALU.mult))
                link(nc.vector.tensor_tensor(small[:, 12:13], small[:, 0:1], small[:, 5:6], ALU.mult))
                nc.vector.tensor_tensor(small[:, 1:2], bn_bias[l], small[:, 12:13], ALU.subtract).then_inc(s_norm, 1)
                dve.wait_ge(s_norm, l + 1)

            link(nc.vector.tensor_tensor(small[:, 15:16], small[:, 0:1], q_gain, ALU.mult))
            nc.vector.tensor_scalar(m_proj[:, :], pick, small[:, 15:16], None, ALU.mult).then_inc(s_pick, 1)
            link(nc.vector.tensor_tensor(small[:, 16:17], small[:, 1:2], q_gain, ALU.mult))
            dve.wait_ge(s_proj, 1)
            nc.vector.tensor_scalar(small[:, 14:15], bank(4)[:, 0:1], q_bias, None, ALU.add).then_inc(s_pick, 1)

        @block.tensor
        def _(pe):
            pe.wait_ge(s_const, 80)
            by_x = l_turned.rearrange("p (i x) -> p i x", x=S)
            for h in range(2):
                nc.tensor.matmul(bank(0)[64 * h:64 * h + 64, :], fwd_y, by_x[:, :, Q * h:Q * (h + 1)],
                                 start=True, stop=True).then_inc(s_lift, 1)
            pe.wait_ge(s_lyt, 1)
            for ri in range(2):
                last = nc.tensor.matmul(bank(1)[:, 0:MODES * PAIRS], fwd_x[ri],
                                        l_yt[:, MODES * PAIRS * ri:MODES * PAIRS * (ri + 1)], start=ri == 0, stop=ri == 1)
            last.then_inc(s_lift, 1)
            nc.tensor.matmul(bank(2)[:, 0:P], lift_w, conv_w[0], start=True, stop=True).then_inc(s_lift, 1)
            for l in range(L):
                def forward_y(n, par):
                    at_least(pe, s_fyt, n - 1 + PAIRS * (l - 1))
                    for h in range(2):
                        pe.wait_ge(s_ftr, 2 * n + h + 1 + 2 * PAIRS * (l - 1))
                        for k in range(2):
                            last = nc.tensor.matmul(bank(2 * par + k)[64 * h:64 * h + 64, :], fwd_y,
                                                    f_tr[h][:, 512 * k:512 * (k + 1)], start=True, stop=True)
                        last.then_inc(s_fy, 1)

                def forward_x(n, par):
                    pe.wait_ge(s_fyt, n + 1 + PAIRS * (l - 1))
                    at_least(pe, s_spec, n - 1 + PAIRS * (l - 1))
                    for ri in range(2):
                        last = nc.tensor.matmul(bank(4 + par)[:, 0:YR], fwd_x[ri], f_yt[:, YR * ri:YR * (ri + 1)],
                                                start=ri == 0, stop=ri == 1)
                    last.then_inc(s_fx, 1)

                if l:
                    pe.wait_ge(s_norm, l)
                    forward_y(0, 0)
                    forward_y(1, 1)
                    forward_x(0, 0)
                    for n in range(2, 4):
                        forward_y(n, n % 2)
                        forward_x(n - 1, (n - 1) % 2)
                    with pe.Fori(2, PAIRS // 2) as it:
                        for par in range(2):
                            forward_y(2 * it + par, par)
                            forward_x(2 * it + par - 1, 1 - par)
                    forward_x(PAIRS - 1, 1)
                    pe.wait_ge(s_spec, PAIRS * l)
                else:
                    pe.wait_ge(s_lyt, 2)
                    pe.wait_ge(s_lspec, 1)

                for ky in range(MODES):
                    n = l * MODES + ky
                    pe.wait_ge(s_min, n + 1)
                    pe.wait_ge(s_rky, 2 * (n + 1))
                    at_least(pe, s_mout, 4 * (n - 1))
                    for kx in range(KXJ):
                        for jh in range(2):
                            for jj in range(2):
                                j, k12 = 2 * jj + jh, KXJ * jh + kx
                                rows = slice(64 * jj, 64 * (jj + 1))
                                at = 512 * (4 * (n % 2) + j) + 2 * CH * kx
                                last = nc.tensor.matmul(ps[Q * j:Q * (j + 1), at:at + 2 * CH],
                                                        m_in[n % 2][rows, Q * k12:Q * (k12 + 1)],
                                                        r_ky[rows, n % RBUF, k12].rearrange("p s o -> p (s o)"),
                                                        start=True, stop=True, tile_position=(64 * jj, Q * j))
                    last.then_inc(s_mix, 1)

                vk = spec[:, :, :].rearrange("p k n -> p (k n)").rearrange("p (k b i o) -> p k b i o", b=2, i=PAIRS, o=CH)

                def inverse_x(n):
                    at_least(pe, s_gs, 2 * n + 2 * PAIRS * l)
                    for p in range(2):
                        last = nc.tensor.matmul(bank(p)[:, 0:YR], inv_x[p], vk[:, :, :, bass.ds(n, 1), :].rearrange("p k b i o -> p k b (i o)"),
                                                start=True, stop=True)
                    last.then_inc(s_gx, 1)

                def pair(n, par):
                    pe.wait_ge(s_gt, n + 1 + PAIRS * l)
                    for h in range(2):
                        half = 2 * n + h + 2 * PAIRS * l
                        at_least(pe, s_x1, half)
                        for k in range(2):
                            last = nc.tensor.matmul(bank(2 + k), inv_y[h], b_gt[par][:, 512 * k:512 * (k + 1)],
                                                    start=True, stop=True)
                        last.then_inc(s_iy, 1)
                        if l:
                            pe.wait_ge(s_bact, half + 1 - 2 * PAIRS)
                        else:
                            pe.wait_ge(s_feat[h], 16 * n + 32)
                        at_least(pe, s_v, half - 1)
                        for k in range(2):
                            last = nc.tensor.matmul(bank(4 + 2 * h + k), conv_w[l] if l else lift_w, b_act[h][:, 512 * k:512 * (k + 1)],
                                                    start=True, stop=True)
                        last.then_inc(s_conv, 1)

                pe.wait_ge(s_msp, (MODES // 2) * (l + 1))
                inverse_x(0)
                inverse_x(1)
                pair(0, 0)
                inverse_x(2)
                pair(1, 1)
                with pe.Fori(1, PAIRS // 2 - 1) as it:
                    for par in range(2):
                        inverse_x(2 * it + par + 1)
                        pair(2 * it + par, par)
                inverse_x(PAIRS - 1)
                pair(PAIRS - 2, 0)
                pair(PAIRS - 1, 1)

                pe.wait_ge(s_bn, 3 * l + 1)
                nc.tensor.matmul(bank(0)[:, 0:2], average, small[:, 2:4], start=True, stop=True).then_inc(s_avg, 1)
                pe.wait_ge(s_bn, 3 * l + 2)
                nc.tensor.matmul(bank(1)[:, 0:1], average, small[:, 4:5], start=True, stop=True).then_inc(s_avg, 1)

            pe.wait_ge(s_chain, CHAIN_AT_PROJ)
            nc.tensor.matmul(bank(4)[:, 0:1], first, small[:, 16:17], start=True, stop=True).then_inc(s_proj, 1)
            pe.wait_ge(s_pick, 1)
            for i in range(PAIRS):
                at_least(pe, s_u, i - 3)
                for k in range(4):
                    last = nc.tensor.matmul(bank(i % 4)[Q * k:Q * (k + 1), :], m_proj[:, :], V[:, BLK * i + 512 * k:BLK * i + 512 * (k + 1)],
                                            start=True, stop=True)
                last.then_inc(s_proj, 1)


DEPTH = 4
EMB = 64
HEADS = 8
DH = EMB // HEADS
FF = 4 * EMB
TILES = BATCH * S // P
GROUPS = 4
GT = TILES // GROUPS
GP = GT // 2
GH = GT * HEADS
GW = GT * EMB
EXPERTS = 4
HID = 128
W_QV, W_K, W_O, W_1, W_2 = 0, 256, 384, 512, 1024
W_LN, W_B1, W_BO, W_B2, W_LAYER = 1152, 1156, 1158, 1222, 1286
E_1, E_2, E_3, E_S1, E_S2, E_S3 = 0, 1024, 1280, 1536, 1664, 1920
E_G, E_B1, E_B2, E_SB1, E_SB2, E_GB, E_B3, E_SB3, E_ALL = 1984, 1992, 1996, 1998, 1999, 2000, 2004, 2260, 2324


def token_layout(Wq, Wk, Wv, Wo, bo, ln1_g, ln1_b, W1, b1, W2, b2, ln2_g, ln2_b):
    out = np.zeros((DEPTH, P, W_LAYER), np.float32)
    for l in range(DEPTH):
        for par in range(2):
            rows = slice(EMB * par, EMB * (par + 1))
            cols = EMB * par
            out[l, rows, W_QV + cols:W_QV + cols + EMB] = Wq[l]
            out[l, rows, W_QV + P + cols:W_QV + P + cols + EMB] = Wv[l]
            out[l, rows, W_K + cols:W_K + cols + EMB] = Wk[l]
            out[l, rows, W_O + cols:W_O + cols + EMB] = Wo[l]
            out[l, rows, W_1 + FF * par:W_1 + FF * (par + 1)] = W1[l]
            for i, v in enumerate((ln1_g, ln1_b, ln2_g, ln2_b)):
                out[l, rows, W_LN + i] = v[l]
        for c in range(2):
            out[l, :, W_2 + EMB * c:W_2 + EMB * (c + 1)] = W2[l, P * c:P * (c + 1)]
            out[l, :, W_B1 + c] = b1[l, P * c:P * (c + 1)]
        out[l, :, W_BO:W_BO + EMB] = bo[l]
        out[l, :, W_B2:W_B2 + EMB] = b2[l]
    return out


def mixture_layout(sW1, sb1, sW2, sb2, sW3, sb3, eW1, eb1, eW2, eb2, eW3, eb3, gW, gb):
    out = np.zeros((P, E_ALL), np.float32)
    for par in range(2):
        rows = slice(EMB * par, EMB * (par + 1))
        for e in range(EXPERTS):
            at = E_1 + HID * (2 * e + par)
            out[rows, at:at + HID] = eW1[e]
        out[rows, E_S1 + EMB * par:E_S1 + EMB * (par + 1)] = sW1
        out[rows, E_S2 + P * par:E_S2 + P * (par + 1)] = sW2
        out[rows, E_SB1] = sb1
        out[rows, E_G + EXPERTS * par:E_G + EXPERTS * (par + 1)] = gW
        for ep in range(2):
            out[rows, E_3 + P * ep + EMB * par:E_3 + P * ep + EMB * (par + 1)] = eW3[2 * ep + par]
            out[rows, E_B2 + ep] = eb2[2 * ep + par]
    for e in range(EXPERTS):
        out[:, E_2 + EMB * e:E_2 + EMB * (e + 1)] = eW2[e]
        out[:, E_B1 + e] = eb1[e]
        out[:, E_B3 + EMB * e:E_B3 + EMB * (e + 1)] = eb3[e]
    out[:, E_S3:E_S3 + EMB] = sW3
    out[:, E_SB2] = sb2
    out[:, E_SB3:E_SB3 + EMB] = sb3
    out[:, E_GB:E_GB + EXPERTS] = gb
    return out


def token_constants():
    own = np.kron(np.eye(2 * HEADS), np.ones((DH, DH)))
    return np.concatenate([np.eye(P), own], axis=1).astype(np.float32)


def token_kernel(nc, tower_out, layers, mixture, table, out):
    f32 = mybir.dt.float32
    ALU = mybir.AluOpType
    ACT = mybir.ActivationFunctionType
    X_AXIS = mybir.AxisListType.X
    SCALE = DH ** -0.25
    G = GROUPS
    NX = TILES * EMB

    with ExitStack() as ctx:
        def sb(name, shape):
            return ctx.enter_context(nc.sbuf_tensor(name, shape, f32))

        def sem(name):
            return ctx.enter_context(nc.semaphore(name))

        u0 = sb("u0", [P, NX])
        xr = sb("xr", [P, NX])
        xb = sb("xb", [P, NX])
        cen = sb("cen", [P, NX])
        sq = sb("sq", [P, NX])
        nrm = sb("nrm", [P, NX])
        hT = sb("hT", [P, NX])
        qs = sb("qs", [P, NX])
        qe = sb("qe", [P, NX])
        ks = sb("ks", [P, NX])
        ke = sb("ke", [P, NX])
        kqT = sb("kqT", [P, GROUPS, 2, GW])
        vd = sb("vd", [P, 2 * NX])
        cx = sb("cx", [P, 2 * NX])
        oT = sb("oT", [P, NX])
        gl = sb("gl", [P, 4 * NX])
        wl = sb("wl", [P, 2, W_LAYER])
        wm = sb("wm", [P, E_ALL])
        cst = sb("cst", [P, 2 * P])
        st = sb("st", [P, 12, TILES])
        hst = sb("hst", [P, 4, TILES * HEADS])
        kst = sb("kst", [P, 4, TILES])
        gates = sb("gates", [P, 8, TILES * EXPERTS])
        ps = ctx.enter_context(nc.psum_tensor("tps", [P, 4096], f32))
        ident, own = cst[:, 0:P], cst[:, P:2 * P]

        def bank(g, i, at=0, n=GW):
            return ps[:, 512 * (2 * g + i) + at:512 * (2 * g + i) + at + n]

        def part(a, g, k=1):
            return a[:, k * GW * g:k * GW * (g + 1)]

        def stat(i, g):
            return st[:, i, GT * g:GT * (g + 1)]

        s_u = sem("s_tokens")
        s_wl = [sem("s_wl0"), sem("s_wl1")]
        s_wm = sem("s_wm")
        s_cst = sem("s_cst")
        s_vzero = sem("s_vzero")
        s_link = sem("s_link")
        s_cen = sem("s_cen")
        s_sq = sem("s_sq")
        s_var = sem("s_var")
        s_dev = sem("s_dev")
        s_nrm = sem("s_nrm")
        s_tr = sem("s_tr")
        s_hT = sem("s_hT")
        s_qkv = sem("s_qkv")
        s_vd = sem("s_vd")
        s_ks = sem("s_ks")
        s_qs = sem("s_qs")
        s_ke = sem("s_ke")
        s_qe = sem("s_qe")
        s_kn = sem("s_kn")
        s_qn = sem("s_qn")
        s_qtp = sem("s_qtp")
        s_qT = sem("s_qT")
        s_ctx = sem("s_ctx")
        s_cx = sem("s_cx")
        s_otp = sem("s_otp")
        s_oT = sem("s_oT")
        s_wo = sem("s_wo")
        s_xb = sem("s_xb")
        s_x = sem("s_x")
        s_ff = sem("s_ff")
        s_gl = sem("s_gl")
        s_ff2 = sem("s_ff2")
        s_gate = sem("s_gate")
        s_coef = sem("s_coef")
        s_m1 = sem("s_m1")
        s_m1a = sem("s_m1a")
        s_m1v = sem("s_m1v")
        s_m2 = sem("s_m2")
        s_m2a = sem("s_m2a")
        s_m2v = sem("s_m2v")
        s_m3 = sem("s_m3")
        s_m3b = sem("s_m3b")
        s_sh1 = sem("s_sh1")
        s_sh2 = sem("s_sh2")
        s_gexp = sem("s_gexp")
        s_glog = sem("s_glog")
        s_out = sem("s_done")

        h1 = sb("h1", [P, 18 * 512])
        h2 = sb("h2", [P, 12 * 512])

        def hidden_1(i):
            bias = wm[:, E_B1 + i // 4:E_B1 + i // 4 + 1] if i < 16 else wm[:, E_SB1:E_SB1 + 1]
            return h1[:, 512 * i:512 * (i + 1)], bias

        def hidden_2(i):
            bias = wm[:, E_B2 + i // 4:E_B2 + i // 4 + 1] if i < 8 else wm[:, E_SB2:E_SB2 + 1]
            return h2[:, 512 * i:512 * (i + 1)], bias

        block = ctx.enter_context(nc.Block())

        def norm_index(l, which):
            return (2 * l + which) * G

        LAST = 2 * DEPTH

        @block.sync
        def _(sp):
            sp.dma_start(cst[:, :], table).then_inc(s_cst, 16)
            u_view = u0[:, :].rearrange("p (t y) -> p t y", y=S)
            for k in range(4):
                for b2 in range(2):
                    for yh in range(2):
                        row = 4 * k + 2 * b2 + yh
                        sp.dma_start(u_view[S * b2 + 16 * k:S * b2 + 16 * (k + 1), :, yh * Q:(yh + 1) * Q],
                                     tower_out[row].rearrange("(i x y) -> x i y", i=PAIRS, x=16)).then_inc(s_u, 16)
            for l in range(DEPTH):
                if l >= 2:
                    sp.wait_ge(s_x, 2 * G * (l - 1))
                sp.dma_start(wl[:, l % 2, :], layers[l]).then_inc(s_wl[l % 2], 16)
            sp.dma_start(wm[:, :], mixture).then_inc(s_wm, 16)
            for g in range(G):
                sp.wait_ge(s_nrm, norm_index(DEPTH, 1) + g + 1)
                sp.dma_start(out[2 * GT * g:2 * GT * (g + 1)].rearrange("(t b) x y -> (b x) t y", b=2),
                             part(nrm, g).rearrange("p (t y) -> p t y", y=S)).then_inc(s_out, 16)
            sp.wait_ge(s_out, 16 * G)

        @block.gpsimd
        def _(pool):
            nc.gpsimd.memset(vd[:, :], 0.0).then_inc(s_vzero, 1)
            for l in range(DEPTH):
                pool.wait_ge(s_wl[l % 2], 16 * (l // 2 + 1))
                for which, at in enumerate((W_BO, W_B2)):
                    bias = wl[:, l % 2, at:at + EMB].unsqueeze(1).broadcast_to([P, GT, EMB])
                    for g in range(G):
                        n = norm_index(l, which)
                        if n:
                            pool.wait_ge(s_x, n - G + g + 1)
                        else:
                            pool.wait_ge(s_u, 256)
                        src = part(xr if n else u0, g)
                        nc.gpsimd.tensor_tensor(part(xb, g).rearrange("p (t e) -> p t e", e=EMB),
                                                src.rearrange("p (t e) -> p t e", e=EMB), bias, ALU.add).then_inc(s_xb, 1)

        @block.scalar
        def _(act):
            def square_root(n):
                for g in range(G):
                    act.wait_ge(s_cen, n + g + 1)
                    nc.scalar.activation(part(sq, g), part(cen, g), ACT.Square).then_inc(s_sq, 1)
                for g in range(G):
                    act.wait_ge(s_var, n + g + 1)
                    nc.scalar.activation(stat(3, g), stat(4, g), ACT.Sqrt, bias=st[:, 2, 0:1], scale=1.0 / EMB).then_inc(s_dev, 1)

            def transposed(n, l, which):
                for g in range(G):
                    act.wait_ge(s_tr, n + g + 1)
                    w = wl[:, l % 2, W_LN + 2 * which:W_LN + 2 * which + 2]
                    nc.scalar.activation(part(hT, g), bank(g, 0), ACT.Identity, bias=w[:, 1:2],
                                         scale=w[:, 0:1]).then_inc(s_hT, 1)

            act.wait_ge(s_vzero, 1)
            for l in range(DEPTH):
                n = norm_index(l, 0)
                square_root(n)
                act.wait_ge(s_wl[l % 2], 16 * (l // 2 + 1))
                transposed(n, l, 0)
                for g in range(G):
                    act.wait_ge(s_qkv, l * G + g + 1)
                    for b in range(2):
                        rows = slice(S * b, S * (b + 1))
                        dst = part(vd, g, 2)[rows].rearrange("p (t h c) -> p t h c", h=2, c=P)[:, :, b]
                        src = bank(g, 0)[rows].rearrange("p (t c) -> p t c", c=P)
                        nc.scalar.copy(dst, src).then_inc(s_vd, 1)
                for g in range(G):
                    act.wait_ge(s_ks, l * G + g + 1)
                    nc.scalar.activation(part(ke, g), part(ks, g), ACT.Exp, scale=SCALE).then_inc(s_ke, 1)
                    act.wait_ge(s_qs, l * G + g + 1)
                    nc.scalar.activation(part(qe, g), part(qs, g), ACT.Exp, scale=SCALE).then_inc(s_qe, 1)
                for g in range(G):
                    act.wait_ge(s_qtp, l * G + g + 1)
                    nc.scalar.copy(kqT[:, g].rearrange("p a n -> p (a n)"), bank(g, 0, 0, 2 * GW)).then_inc(s_qT, 1)
                for g in range(G):
                    act.wait_ge(s_otp, l * G + g + 1)
                    nc.scalar.copy(part(oT, g), bank(g, 0)).then_inc(s_oT, 1)
                n = norm_index(l, 1)
                square_root(n)
                transposed(n, l, 1)
                for g in range(G):
                    for c in range(2):
                        act.wait_ge(s_ff, 2 * (l * G + g) + c + 1)
                        nc.scalar.activation(part(gl, g, 4)[:, 2 * GW * c:2 * GW * (c + 1)], bank(g, c, 0, 2 * GW), ACT.Gelu,
                                             bias=wl[:, l % 2, W_B1 + c:W_B1 + c + 1]).then_inc(s_gl, 1)
            n = norm_index(DEPTH, 0)
            square_root(n)
            for g in range(G):
                act.wait_ge(s_tr, n + g + 1)
                nc.scalar.copy(part(hT, g), bank(g, 0)).then_inc(s_hT, 1)
            act.wait_ge(s_glog, 1)
            nc.scalar.activation(gates[:, 1, :], gates[:, 0, :], ACT.Exp).then_inc(s_gexp, 1)
            act.wait_ge(s_wm, 16)
            for i in range(0, 18, 2):
                act.wait_ge(s_m1, i + 1)
                dst, bias = hidden_1(i)
                nc.scalar.activation(dst, ps[:, 512 * (i % 8):512 * (i % 8 + 1)], ACT.Relu, bias=bias).then_inc(s_m1a, 1)
            for i in range(0, 12, 2):
                act.wait_ge(s_m2, i + 1)
                dst, bias = hidden_2(i)
                nc.scalar.activation(dst, ps[:, 512 * ((i + 18) % 8):512 * ((i + 18) % 8 + 1)], ACT.Relu,
                                     bias=bias).then_inc(s_m2a, 1)
            act.wait_ge(s_gexp, 2)
            nc.scalar.activation(st[:, 8, :], st[:, 7, :], ACT.Exp).then_inc(s_gexp, 1)
            square_root(norm_index(DEPTH, 1))

        @block.vector
        def _(dve):
            chain = [0]

            def link(ins):
                chain[0] += 1
                ins.then_inc(s_link, 1)
                dve.wait_ge(s_link, chain[0])

            def normalise(n, src, ready):
                for g in range(G):
                    ready(g)
                    x3 = part(src, g).rearrange("p (t e) -> p t e", e=EMB)
                    link(nc.vector.reduce_sum(stat(0, g), x3, X_AXIS))
                    if n:
                        dve.wait_ge(s_nrm, n - G + g + 1)
                    nc.vector.scalar_tensor_tensor(out=part(cen, g).rearrange("p (t e) -> p t e", e=EMB), in0=x3,
                                                   scalar=float(EMB), in1=stat(0, g).unsqueeze(2).broadcast_to([P, GT, EMB]),
                                                   op0=ALU.mult, op1=ALU.subtract).then_inc(s_cen, 1)
                for g in range(G):
                    dve.wait_ge(s_sq, n + g + 1)
                    nc.vector.reduce_sum(stat(4, g), part(sq, g).rearrange("p (t e) -> p t e", e=EMB), X_AXIS).then_inc(s_var, 1)
                for g in range(G):
                    dve.wait_ge(s_dev, n + g + 1)
                    link(nc.vector.reciprocal(stat(5, g), stat(3, g)))
                    nc.vector.tensor_tensor(part(nrm, g).rearrange("p (t e) -> p t e", e=EMB),
                                            part(cen, g).rearrange("p (t e) -> p t e", e=EMB),
                                            stat(5, g).unsqueeze(2).broadcast_to([P, GT, EMB]), ALU.mult).then_inc(s_nrm, 1)

            def residual(n, b, done, count):
                for g in range(G):
                    dve.wait_ge(done, count + g + 1)
                    dve.wait_ge(s_xb, n + g + 1)
                    nc.vector.tensor_tensor(part(xr, g), bank(g, b), part(xb, g), ALU.add).then_inc(s_x, 1)

            link(nc.vector.memset(st[:, 2, :], EMB * EMB * EPS))
            for l in range(DEPTH):
                n = norm_index(l, 0)
                if l:
                    normalise(n, xr, lambda g: dve.wait_ge(s_x, n - G + g + 1))
                else:
                    dve.wait_ge(s_u, 256)
                    normalise(0, u0, lambda g: None)
                for g in range(G):
                    dve.wait_ge(s_qkv, l * G + g + 1)
                    k3 = bank(g, 1).rearrange("p (i n) -> p i n", n=S)
                    kmax, hmax = kst[:, 0, GT * g:GT * (g + 1)], hst[:, 0, GH * g:GH * (g + 1)]
                    link(nc.vector.reduce_max(kmax, k3, X_AXIS))
                    nc.vector.tensor_tensor(part(ks, g).rearrange("p (i n) -> p i n", n=S), k3,
                                            kmax.unsqueeze(2).broadcast_to([P, GT, S]), ALU.subtract).then_inc(s_ks, 1)
                    q4 = bank(g, 1, GW).rearrange("p (t h d) -> p t h d", h=2 * HEADS, d=DH)
                    hm = hmax.rearrange("p (t h) -> p t h", h=2 * HEADS)
                    link(nc.vector.reduce_max(hm, q4, X_AXIS))
                    nc.vector.tensor_tensor(part(qs, g).rearrange("p (t h d) -> p t h d", h=2 * HEADS, d=DH), q4,
                                            hm.unsqueeze(3).broadcast_to([P, GP, 2 * HEADS, DH]), ALU.subtract).then_inc(s_qs, 1)
                for g in range(G):
                    dve.wait_ge(s_ke, l * G + g + 1)
                    k3 = part(ke, g).rearrange("p (i n) -> p i n", n=S)
                    ksum, krec = kst[:, 1, GT * g:GT * (g + 1)], kst[:, 2, GT * g:GT * (g + 1)]
                    link(nc.vector.reduce_sum(ksum, k3, X_AXIS))
                    link(nc.vector.reciprocal(krec, ksum))
                    nc.vector.tensor_tensor(part(ks, g).rearrange("p (i n) -> p i n", n=S), k3,
                                            krec.unsqueeze(2).broadcast_to([P, GT, S]), ALU.mult).then_inc(s_kn, 1)
                    dve.wait_ge(s_qe, l * G + g + 1)
                    q3 = part(qe, g).rearrange("p (h d) -> p h d", d=DH)
                    hsum, hrec = hst[:, 1, GH * g:GH * (g + 1)], hst[:, 2, GH * g:GH * (g + 1)]
                    link(nc.vector.reduce_sum(hsum, q3, X_AXIS))
                    link(nc.vector.reciprocal(hrec, hsum))
                    nc.vector.tensor_tensor(part(qs, g).rearrange("p (h d) -> p h d", d=DH), q3,
                                            hrec.unsqueeze(2).broadcast_to([P, GH, DH]), ALU.mult).then_inc(s_qn, 1)
                for g in range(G):
                    dve.wait_ge(s_ctx, l * G + g + 1)
                    nc.vector.tensor_tensor(part(cx, g, 2).rearrange("p (i c) -> p i c", c=P),
                                            bank(g, 1, 0, 2 * GW).rearrange("p (i c) -> p i c", c=P),
                                            own.unsqueeze(1).broadcast_to([P, GT, P]), ALU.mult).then_inc(s_cx, 1)
                residual(n, 1, s_wo, l * G)
                n = norm_index(l, 1)
                normalise(n, xr, lambda g: dve.wait_ge(s_x, n - G + g + 1))
                residual(n, 0, s_ff2, l * G)
            n = norm_index(DEPTH, 0)
            dve.wait_ge(s_x, n)
            link(nc.vector.tensor_tensor(xr[:, :], xr[:, :], u0[:, :], ALU.add))
            normalise(n, xr, lambda g: None)

            dve.wait_ge(s_gate, 1)
            dve.wait_ge(s_wm, 16)
            te = [P, TILES, EXPERTS]

            def gate(i):
                return gates[:, i, :].rearrange("p (t e) -> p t e", e=EXPERTS)

            def spread(i):
                return st[:, i, :].unsqueeze(2).broadcast_to(te)

            link(nc.vector.tensor_tensor(gate(2), ps[:, 0:TILES * EXPERTS].rearrange("p (t e) -> p t e", e=EXPERTS),
                                         wm[:, E_GB:E_GB + EXPERTS].unsqueeze(1).broadcast_to(te), ALU.add))
            link(nc.vector.reduce_max(st[:, 9, :], gate(2), X_AXIS))
            nc.vector.tensor_tensor(gate(0), gate(2), spread(9), ALU.subtract).then_inc(s_glog, 1)
            dve.wait_ge(s_gexp, 1)
            link(nc.vector.reduce_sum(st[:, 9, :], gate(1), X_AXIS))
            link(nc.vector.reciprocal(st[:, 10, :], st[:, 9, :]))
            link(nc.vector.tensor_tensor(gate(2), gate(1), spread(10), ALU.mult))

            def pick_first(values, best, chosen, equal, left):
                link(nc.vector.reduce_max(st[:, best, :], gate(values), X_AXIS))
                link(nc.vector.tensor_tensor(gate(equal), gate(values), spread(best), ALU.is_ge))
                link(nc.vector.memset(st[:, left, :], 1.0))
                for e in range(EXPERTS):
                    link(nc.vector.tensor_tensor(gate(chosen)[:, :, e], gate(equal)[:, :, e], st[:, left, :], ALU.mult))
                    link(nc.vector.tensor_tensor(st[:, left, :], st[:, left, :], gate(chosen)[:, :, e], ALU.subtract))

            pick_first(2, 9, 3, 4, 11)
            link(nc.vector.scalar_tensor_tensor(out=gates[:, 5, :], in0=gates[:, 3, :], scalar=-2.0, in1=gates[:, 2, :],
                                                op0=ALU.mult, op1=ALU.add))
            pick_first(5, 10, 6, 4, 11)
            nc.vector.tensor_tensor(st[:, 7, :], st[:, 10, :], st[:, 9, :], ALU.subtract).then_inc(s_gexp, 1)

            for i in range(1, 18, 2):
                dve.wait_ge(s_m1, i + 1)
                dst, bias = hidden_1(i)
                nc.vector.tensor_scalar(dst, ps[:, 512 * (i % 8):512 * (i % 8 + 1)], bias, 0.0, ALU.add, ALU.max).then_inc(s_m1v, 1)
            for i in range(1, 12, 2):
                dve.wait_ge(s_m2, i + 1)
                dst, bias = hidden_2(i)
                nc.vector.tensor_scalar(dst, ps[:, 512 * ((i + 18) % 8):512 * ((i + 18) % 8 + 1)], bias, 0.0,
                                        ALU.add, ALU.max).then_inc(s_m2v, 1)

            dve.wait_ge(s_gexp, 3)
            link(nc.vector.tensor_scalar(st[:, 9, :], st[:, 8, :], 1.0, None, ALU.add))
            link(nc.vector.reciprocal(st[:, 10, :], st[:, 9, :]))
            link(nc.vector.tensor_tensor(gate(4), gate(6), spread(8), ALU.mult))
            link(nc.vector.tensor_tensor(gate(4), gate(4), gate(3), ALU.add))
            link(nc.vector.tensor_tensor(gate(7), gate(4), spread(10), ALU.mult))

            link(nc.vector.tensor_tensor(xr[:, :].rearrange("p (t e) -> p t e", e=EMB), nrm[:, :].rearrange("p (t e) -> p t e", e=EMB),
                                         wm[:, E_SB3:E_SB3 + EMB].unsqueeze(1).broadcast_to([P, TILES, EMB]), ALU.add))
            four = [P, 2, EXPERTS, EMB]
            for t in range(TILES // 2):
                dve.wait_ge(s_m3, t + 1)
                pick = gl[:, 512 * (t % 2):512 * (t % 2 + 1)]
                p4 = pick.rearrange("p (t e c) -> p t e c", t=2, c=EMB)
                src = ps[:, 512 * (t % 4):512 * (t % 4 + 1)].rearrange("p (t e c) -> p t e c", t=2, c=EMB)
                bias = wm[:, E_B3:E_B3 + EXPERTS * EMB].rearrange("p (e c) -> p e c", c=EMB).unsqueeze(1).broadcast_to(four)
                nc.vector.tensor_tensor(p4, src, bias, ALU.add).then_inc(s_m3b, 1)
                dve.wait_ge(s_m3b, t + 1)
                coef = gate(7)[:, 2 * t:2 * t + 2, :].unsqueeze(3).broadcast_to(four)
                link(nc.vector.tensor_tensor(p4, p4, coef, ALU.mult))
                link(nc.vector.reduce_sum(sq[:, P * t:P * (t + 1)].rearrange("p (t c) -> p t c", c=EMB),
                                          pick.rearrange("p (t e c) -> p t c e", t=2, c=EMB), X_AXIS))
            dve.wait_ge(s_sh2, 2)
            link(nc.vector.tensor_tensor(xr[:, :], xr[:, :], sq[:, :], ALU.add))
            link(nc.vector.tensor_tensor(xr[:, :], xr[:, :], ps[:, 2048:2048 + NX], ALU.add))
            normalise(norm_index(DEPTH, 1), xr, lambda g: None)

        @block.tensor
        def _(pe):
            def transposes(n):
                for g in range(G):
                    pe.wait_ge(s_nrm, n + g + 1)
                    for t in range(GP):
                        last = nc.tensor.transpose(bank(g, 0)[:, P * t:P * (t + 1)], part(nrm, g)[:, P * t:P * (t + 1)], ident)
                    last.then_inc(s_tr, 1)

            pe.wait_ge(s_cst, 16)
            for l in range(DEPTH):
                w = wl[:, l % 2, :]
                n = norm_index(l, 0)
                transposes(n)
                pe.wait_ge(s_wl[l % 2], 16 * (l // 2 + 1))
                for g in range(G):
                    pe.wait_ge(s_hT, n + g + 1)
                    h = part(hT, g)
                    nc.tensor.matmul(bank(g, 1), w[:, W_K:W_K + P], h, start=True, stop=True)
                    for t in range(GP):
                        for i in range(2):
                            last = nc.tensor.matmul(bank(g, 1 - i, GW * (1 - i))[:, P * t:P * (t + 1)], h[:, P * t:P * (t + 1)],
                                                    w[:, W_QV + P * i:W_QV + P * (i + 1)], start=True, stop=True)
                    last.then_inc(s_qkv, 1)
                for g in range(G):
                    pe.wait_ge(s_vd, 2 * (l * G + g + 1))
                    pe.wait_ge(s_kn, l * G + g + 1)
                    for t in range(GP):
                        nc.tensor.transpose(bank(g, 0)[:, P * t:P * (t + 1)], part(ks, g)[:, P * t:P * (t + 1)], ident)
                    pe.wait_ge(s_qn, l * G + g + 1)
                    for t in range(GP):
                        last = nc.tensor.transpose(bank(g, 0, GW)[:, P * t:P * (t + 1)], part(qs, g)[:, P * t:P * (t + 1)], ident)
                    last.then_inc(s_qtp, 1)
                for g in range(G):
                    pe.wait_ge(s_qT, l * G + g + 1)
                    for t in range(GP):
                        last = nc.tensor.matmul(bank(g, 1, 2 * P * t, 2 * P), kqT[:, g, 0, P * t:P * (t + 1)],
                                                part(vd, g, 2)[:, 2 * P * t:2 * P * (t + 1)], start=True, stop=True)
                    last.then_inc(s_ctx, 1)
                for g in range(G):
                    pe.wait_ge(s_cx, l * G + g + 1)
                    for i in range(GT):
                        last = nc.tensor.matmul(bank(g, 0)[:, S * i:S * (i + 1)], part(cx, g, 2)[:, P * i:P * (i + 1)],
                                                kqT[:, g, 1, S * i:S * (i + 1)], start=True, stop=True)
                    last.then_inc(s_otp, 1)
                for g in range(G):
                    pe.wait_ge(s_oT, l * G + g + 1)
                    for t in range(GP):
                        last = nc.tensor.matmul(bank(g, 1)[:, P * t:P * (t + 1)], part(oT, g)[:, P * t:P * (t + 1)],
                                                w[:, W_O:W_O + P], start=True, stop=True)
                    last.then_inc(s_wo, 1)
                n = norm_index(l, 1)
                transposes(n)
                for g in range(G):
                    pe.wait_ge(s_hT, n + g + 1)
                    for c in range(2):
                        for par in range(2):
                            at = W_1 + P * (2 * par + c)
                            last = nc.tensor.matmul(bank(g, c, GW * par), w[:, at:at + P], part(hT, g), start=True, stop=True)
                        last.then_inc(s_ff, 1)
                for g in range(G):
                    pe.wait_ge(s_gl, 2 * (l * G + g + 1))
                    for t in range(GT):
                        for c in range(2):
                            at = GW * (2 * c + t % 2) + P * (t // 2)
                            last = nc.tensor.matmul(bank(g, 0)[:, EMB * t:EMB * (t + 1)], part(gl, g, 4)[:, at:at + P],
                                                    w[:, W_2 + EMB * c:W_2 + EMB * (c + 1)], start=c == 0, stop=c == 1)
                    last.then_inc(s_ff2, 1)

            transposes(norm_index(DEPTH, 0))
            pe.wait_ge(s_wm, 16)
            pe.wait_ge(s_hT, norm_index(DEPTH, 1))
            for t in range(TILES // 2):
                last = nc.tensor.matmul(ps[:, 2 * EXPERTS * t:2 * EXPERTS * (t + 1)], hT[:, P * t:P * (t + 1)],
                                        wm[:, E_G:E_G + 2 * EXPERTS], start=True, stop=True)
            last.then_inc(s_gate, 1)
            pe.wait_ge(s_glog, 1)
            for i in range(18):
                if i >= 8:
                    pe.wait_ge(s_m1v if i % 2 else s_m1a, (i - 8) // 2 + 1)
                w = wm[:, E_1 + HID * (i // 2):E_1 + HID * (i // 2 + 1)] if i < 16 else wm[:, E_S1:E_S1 + P]
                nc.tensor.matmul(ps[:, 512 * (i % 8):512 * (i % 8 + 1)], w, hT[:, 512 * (i % 2):512 * (i % 2 + 1)], start=True, stop=True).then_inc(s_m1, 1)
            pe.wait_ge(s_m1v, 9)
            pe.wait_ge(s_m1a, 9)
            for i in range(12):
                if i >= 8:
                    pe.wait_ge(s_m2v if i % 2 else s_m2a, (i - 8) // 2 + 1)
                at = (i + 18) % 8
                if i < 8:
                    for e2 in range(2):
                        e = 2 * (i // 4) + e2
                        src = 4 * e + i % 4
                        last = nc.tensor.matmul(ps[EMB * e2:EMB * (e2 + 1), 512 * at:512 * (at + 1)], wm[:, E_2 + EMB * e:E_2 + EMB * (e + 1)],
                                                h1[:, 512 * src:512 * (src + 1)], start=True, stop=True)
                else:
                    par = (i - 8) // 2
                    last = nc.tensor.matmul(ps[:, 512 * at:512 * (at + 1)], wm[:, E_S2 + P * par:E_S2 + P * (par + 1)],
                                            h1[:, 512 * (16 + i % 2):512 * (17 + i % 2)], start=True, stop=True)
                last.then_inc(s_m2, 1)
            pe.wait_ge(s_m2v, 6)
            pe.wait_ge(s_m2a, 6)

            def place(t):
                return t % 2, t // 8, P * ((t % 8) // 2)

            for half in range(2):
                for t in range(8 * half, 8 * (half + 1)):
                    par, g, col = place(t)
                    at = 512 * (8 + 2 * par + g) + col
                    last = nc.tensor.matmul(ps[:, 2048 + EMB * t:2048 + EMB * (t + 1)], h2[:, at:at + P],
                                            wm[:, E_S3:E_S3 + EMB], start=True, stop=True)
                last.then_inc(s_sh2, 1)
            for t in range(TILES):
                par, g, col = place(t)
                if t % 2 == 0 and t >= 8:
                    pe.wait_ge(s_m3b, (t - 8) // 2 + 1)
                for ep in range(2):
                    at = 512 * (4 * ep + 2 * par + g) + col
                    dst = 512 * ((t // 2) % 4) + 256 * (t % 2) + P * ep
                    last = nc.tensor.matmul(ps[:, dst:dst + P], h2[:, at:at + P], wm[:, E_3 + P * ep:E_3 + P * (ep + 1)],
                                            start=True, stop=True)
                if t % 2:
                    last.then_inc(s_m3, 1)


_TOWER = ["p_w", "p_b", "fw1", "fw2", "w_w", "w_b", "bn_g", "bn_b", "q_w", "q_b"]
_ATTN = ["Wq", "Wk", "Wv", "Wo", "bo", "ln1_g", "ln1_b", "W1", "b1", "W2", "b2", "ln2_g", "ln2_b"]
_FFN = ["sW1", "sb1", "sW2", "sb2", "sW3", "sb3", "eW1", "eb1", "eW2", "eb2", "eW3", "eb3", "gW", "gb"]


def kernel(**inputs):
    import numpy as _np
    import concourse.bacc as _bacc
    from concourse import mybir as _mybir
    from concourse.bass_utils import run_bass_kernel_spmd as _run

    def given(prefix, names):
        return {n: _np.asarray(inputs[prefix + n]) for n in names}

    pixels, turned, weights, lift_rows, modes = tower_layout(_np.asarray(inputs["x"]), **given("L0_tok_", _TOWER))
    table, grid, grid_spectra = constants()
    arrays = {
        "pixels": pixels, "weights": weights, "modes": modes, "table": table, "grid": grid,
        "turned": turned, "lift_rows": lift_rows, "grid_spectra": grid_spectra,
        "layers": token_layout(**given("L0_attn_", _ATTN)),
        "mixture": mixture_layout(**given("L0_ffn_", _FFN)),
        "token_table": token_constants(),
    }
    arrays = {f"in_{k}": _np.ascontiguousarray(v) for k, v in arrays.items()}
    nc = _bacc.Bacc("TRN2", target_bir_lowering=False, num_devices=1)
    f32 = _mybir.dt.float32
    a = {k: nc.dram_tensor(k, v.shape, f32, kind="ExternalInput").ap() for k, v in arrays.items()}
    out = nc.dram_tensor("out_dram", (BATCH, S, S), f32, kind="ExternalOutput").ap()
    scratch = nc.dram_tensor("tower_out", (16, PAIRS * 512), f32, kind="Internal").ap()
    tower_kernel(nc, *(a["in_" + k] for k in ("pixels", "turned", "weights", "lift_rows", "modes", "table", "grid",
                                              "grid_spectra")), scratch)
    token_kernel(nc, scratch, a["in_layers"], a["in_mixture"], a["in_token_table"], out)
    r = _run(nc, [arrays], core_ids=[0])
    return r.results[0]["out_dram"]
```
